# Optimizing a Trainium2 kernel written in Bass

```python
import numpy as np
import jax
import jax.numpy as jnp

def _softmax(x, axis=-1):
    return jax.nn.softmax(x, axis=axis)

def _gelu(x):
    return jax.nn.gelu(x, approximate=True)

def _silu(x):
    return jax.nn.silu(x)

def _sigmoid(x):
    return jax.nn.sigmoid(x)

def _layernorm(x, axis=-1, eps=1e-05):
    m = jnp.mean(x, axis=axis, keepdims=True)
    v = jnp.var(x, axis=axis, keepdims=True)
    return (x - m) / jnp.sqrt(v + eps)

def _scatter_add(tgt, idx, src, axis=0):
    return tgt.at[idx].add(src)

def _segment_sum(src, seg, n):
    return jax.ops.segment_sum(src, seg, n)
kernel_name = 'mk_seq_postln_d1_jaxref_r8_19f16a'

def setup_inputs(seed: int=0):
    np.random.seed(seed)
    _w = jnp.asarray

    def _L0_attn_setup():
        import jax, jax.numpy as jnp
        import numpy as np
        EMBED_DIM = 128
        key = jax.random.key(seed)
        ks = jax.random.split(key, 9)
        B, S, D = (4, 512, EMBED_DIM)
        s = 1.0 / np.sqrt(D)
        inp = {'x': jax.random.normal(ks[0], (B, S, D), dtype=jnp.float32)}
        names = ['q', 'k', 'v', 'out']
        for i, n in enumerate(names):
            inp[f'w_{n}'] = jax.random.uniform(ks[1 + 2 * i], (D, D), jnp.float32, -s, s)
            inp[f'b_{n}'] = jax.random.uniform(ks[2 + 2 * i], (D,), jnp.float32, -s, s)
        return inp
    _L0_attn_in = _L0_attn_setup()

    def _L0_ffn_setup():
        import jax, jax.numpy as jnp
        import numpy as np
        IN_DIM = 128
        HIDDEN = 128
        OUT_DIM = 128
        NUM_EXPERTS = 16
        TOP_K = 2
        ROUTER_TEMP = 1.0
        LN_EPS = 1e-05

        def _layernorm(h, g, b):
            mu = jnp.mean(h, axis=-1, keepdims=True)
            var = jnp.mean(jnp.square(h - mu), axis=-1, keepdims=True)
            return (h - mu) * jax.lax.rsqrt(var + LN_EPS) * g + b
        key = jax.random.key(seed)
        ks = jax.random.split(key, 8)
        s_in = 1.0 / np.sqrt(IN_DIM)
        s_h = 1.0 / np.sqrt(HIDDEN)
        x = jax.random.normal(ks[0], (4, 256, IN_DIM), dtype=jnp.float32)
        Wr = jax.random.uniform(ks[1], (IN_DIM, NUM_EXPERTS), jnp.float32, -s_in, s_in)
        br = jax.random.uniform(ks[2], (NUM_EXPERTS,), jnp.float32, -s_in, s_in)
        W1 = jax.random.uniform(ks[3], (NUM_EXPERTS, IN_DIM, HIDDEN), jnp.float32, -s_in, s_in)
        b1 = jax.random.uniform(ks[4], (NUM_EXPERTS, HIDDEN), jnp.float32, -s_in, s_in)
        g1 = jnp.ones((NUM_EXPERTS, HIDDEN), jnp.float32)
        be1 = jnp.zeros((NUM_EXPERTS, HIDDEN), jnp.float32)
        W2 = jax.random.uniform(ks[5], (NUM_EXPERTS, HIDDEN, OUT_DIM), jnp.float32, -s_h, s_h)
        b2 = jax.random.uniform(ks[6], (NUM_EXPERTS, OUT_DIM), jnp.float32, -s_h, s_h)
        return {'x': x, 'Wr': Wr, 'br': br, 'W1': W1, 'b1': b1, 'g1': g1, 'be1': be1, 'W2': W2, 'b2': b2}
    _L0_ffn_in = _L0_ffn_setup()
    _d = {'L0_attn_x': _L0_attn_in['x'], 'L0_attn_w_q': _L0_attn_in['w_q'], 'L0_attn_b_q': _L0_attn_in['b_q'], 'L0_attn_w_k': _L0_attn_in['w_k'], 'L0_attn_b_k': _L0_attn_in['b_k'], 'L0_attn_w_v': _L0_attn_in['w_v'], 'L0_attn_b_v': _L0_attn_in['b_v'], 'L0_attn_w_out': _L0_attn_in['w_out'], 'L0_attn_b_out': _L0_attn_in['b_out'], 'L0_ffn_Wr': _L0_ffn_in['Wr'], 'L0_ffn_br': _L0_ffn_in['br'], 'L0_ffn_W1': _L0_ffn_in['W1'], 'L0_ffn_b1': _L0_ffn_in['b1'], 'L0_ffn_g1': _L0_ffn_in['g1'], 'L0_ffn_be1': _L0_ffn_in['be1'], 'L0_ffn_W2': _L0_ffn_in['W2'], 'L0_ffn_b2': _L0_ffn_in['b2']}
    _x0 = _d['L0_attn_x']
    _d['L0_attn_x'] = jax.random.normal(jax.random.fold_in(jax.random.key(seed), 1), (8, 1024, 128), dtype=_x0.dtype)
    del _x0
    return _d

def reference(L0_attn_x, L0_attn_w_q, L0_attn_b_q, L0_attn_w_k, L0_attn_b_k, L0_attn_w_v, L0_attn_b_v, L0_attn_w_out, L0_attn_b_out, L0_ffn_Wr, L0_ffn_br, L0_ffn_W1, L0_ffn_b1, L0_ffn_g1, L0_ffn_be1, L0_ffn_W2, L0_ffn_b2):

    def _L0_attn_ref(x, w_q, b_q, w_k, b_k, w_v, b_v, w_out, b_out):
        import jax, jax.numpy as jnp
        import numpy as np
        EMBED_DIM = 128
        D = x.shape[-1]
        scaling = 1.0 / jnp.sqrt(jnp.asarray(D, x.dtype))
        q = jnp.einsum('bsd,ed->bse', x, w_q) + b_q
        k = jnp.einsum('bsd,ed->bse', x, w_k) + b_k
        v = jnp.einsum('bsd,ed->bse', x, w_v) + b_v
        scores = jnp.einsum('bqd,bkd->bqk', q, k) * scaling
        attn = jax.nn.softmax(scores, axis=-1)
        out = jnp.einsum('bqk,bkd->bqd', attn, v)
        return jnp.einsum('bsd,ed->bse', out, w_out) + b_out

    def _L0_ffn_ref(x, Wr, br, W1, b1, g1, be1, W2, b2):
        import jax, jax.numpy as jnp
        import numpy as np
        IN_DIM = 128
        HIDDEN = 128
        OUT_DIM = 128
        NUM_EXPERTS = 16
        TOP_K = 2
        ROUTER_TEMP = 1.0
        LN_EPS = 1e-05

        def _layernorm(h, g, b):
            mu = jnp.mean(h, axis=-1, keepdims=True)
            var = jnp.mean(jnp.square(h - mu), axis=-1, keepdims=True)
            return (h - mu) * jax.lax.rsqrt(var + LN_EPS) * g + b
        orig_shape = x.shape[:-1]
        x_flat = x.reshape(-1, x.shape[-1])
        logits = (x_flat @ Wr + br) / max(ROUTER_TEMP, 1e-06)
        probs = jax.nn.softmax(logits, axis=-1)
        topk_w, topk_idx = jax.lax.top_k(probs, TOP_K)
        topk_w = topk_w / jnp.clip(jnp.sum(topk_w, axis=-1, keepdims=True), 1e-09)
        h = jnp.einsum('nc,ech->neh', x_flat, W1) + b1
        h = _layernorm(h, g1, be1)
        h = jax.nn.gelu(h, approximate=False)
        expert_out = jnp.einsum('neh,eho->neo', h, W2) + b2
        sel = jnp.take_along_axis(expert_out, topk_idx[:, :, None], axis=1)
        y_flat = jnp.sum(sel * topk_w[:, :, None], axis=1)
        return y_flat.reshape(*orig_shape, y_flat.shape[-1])
    x = L0_attn_x
    x = _layernorm(x + _L0_attn_ref(x, L0_attn_w_q, L0_attn_b_q, L0_attn_w_k, L0_attn_b_k, L0_attn_w_v, L0_attn_b_v, L0_attn_w_out, L0_attn_b_out), axis=-1)
    x = _layernorm(x + _L0_ffn_ref(x, L0_ffn_Wr, L0_ffn_br, L0_ffn_W1, L0_ffn_b1, L0_ffn_g1, L0_ffn_be1, L0_ffn_W2, L0_ffn_b2), axis=-1)
    return x

_drawn_inputs = setup_inputs


def setup_inputs(seed=0):
    import zlib

    import numpy as np

    out = dict(_drawn_inputs(seed))
    spreads = {'L0_ffn_g1': (1.0, 0.2), 'L0_ffn_be1': (0.0, 0.292)}
    factors = {'L0_attn_b_q': 21.397, 'L0_attn_b_k': 64.0}
    for name, (base, spread) in spreads.items():
        noise = np.random.default_rng([zlib.crc32(name.encode()), seed]).standard_normal(out[name].shape)
        drawn = base * np.exp(spread * noise) if base else spread * noise
        out[name] = jnp.asarray(drawn.astype(out[name].dtype))
    for name, factor in factors.items():
        out[name] = (out[name] * factor).astype(out[name].dtype)
    return out
```

```python
from contextlib import ExitStack

import concourse.bass as bass
from concourse import mybir

F32 = mybir.dt.float32
F32R = mybir.dt.float32r
BF16 = mybir.dt.bfloat16
I32 = mybir.dt.int32
U32 = mybir.dt.uint32
ALU = mybir.AluOpType
ACT = mybir.ActivationFunctionType
AX = mybir.AxisListType

P = 128
EPS = 1e-5


def wait(engine, sem, value):
    if isinstance(value, int) and value <= 0:
        return
    engine.wait_ge(sem, value)


class Chain:

    def __init__(self, engine, sem):
        self.engine, self.sem, self.base, self.steps = engine, sem, 0, 0

    def then(self, instruction):
        instruction.then_inc(self.sem, 1)
        self.steps += 1

    def sync(self):
        wait(self.engine, self.sem, self.base + self.steps)

    def enter(self, per_iteration, i):
        self.outer, self.per = self.base + self.steps, per_iteration
        self.base, self.steps = self.outer + i * per_iteration, 0

    def leave(self, iterations):
        assert self.steps == self.per, self.steps
        self.base, self.steps = self.outer + iterations * self.per, 0


def post_ln_moe_layer(nc, x, w_q, b_q, w_k, b_k, w_v, b_v, w_out, b_out,
                      w_r, b_r, w_1, b_1, g_1, be_1, w_2, b_2, out):
    NB, S, D = x.shape
    E = w_r.shape[1]
    H = w_1.shape[2]
    N = NB * S
    TILES = S // P
    CHUNK = 4
    CHUNKS = NB * TILES // CHUNK
    CW = CHUNK * P
    KT = S // P
    assert D == P and H == P and TILES == 2 * CHUNK and NB % 2 == 0
    SCALE = float(D) ** -0.5
    REGION = N + P
    ROW = D + 4
    EXPERT_TILES = -(-(2 * N // P + E) // CHUNK) * CHUNK
    GROUPS = EXPERT_TILES // CHUNK
    assert GROUPS % 2 == 0 and EXPERT_TILES <= 2 * P

    with ExitStack() as ctx, ExitStack() as late:
        def sb(name, shape, dt=F32, stack=None):
            return (stack or ctx).enter_context(nc.sbuf_tensor(name, shape, dt))

        def sem(name):
            return ctx.enter_context(nc.semaphore(name))

        routed = nc.dram_tensor("routed_rows", [E * REGION, ROW], F32).ap()
        chosen = nc.dram_tensor("expert_rows", [2 * N, D], F32).ap()
        kept = nc.dram_tensor("attention_rows", [N, D], F32).ap()

        x_v = x.rearrange("n (p j) d -> n p j d", p=P)
        out_v = out.rearrange("n (p c j) d -> n c p j d", p=P, c=2)
        kept_v = kept.rearrange("(n p c j) d -> n c p j d", n=NB, p=P, c=2)
        chosen_v = chosen.rearrange("(n p c j k) d -> n c p j (k d)", n=NB, p=P, c=2, k=2)

        ident = sb("ident", [P, P])
        partition = sb("partition", [P, 1])
        column = sb("column", [P, P])
        expert_ids = sb("expert_ids", [P, E])
        w1_sb = sb("w1_sb", [P, E, H])
        w2_sb = sb("w2_sb", [P, E, D])
        b1_bc = sb("b1_bc", [P, E, H])
        b2_bc = sb("b2_bc", [P, E, D])
        g_rows = sb("g_rows", [E, 2, H])
        g_cols = sb("g_cols", [P, 2, E])
        gates = sb("gates", [P, CHUNKS, CHUNK, 2])
        minus_half = sb("minus_half", [P, CHUNK])
        region_start = sb("region_start", [P, E])
        pad_row = sb("pad_row", [P, ROW])
        base = sb("base", [P, CHUNK + 1, E])
        base_i = sb("base_i", [P, E], I32)
        tile_table = sb("tile_table", [1, 4 * P], I32)
        var = sb("var", [P, 2, CHUNK])
        rstd = sb("rstd", [P, 2, CHUNK])
        stats = sb("stats", [P, 2, CHUNK, 6])
        mean_var = sb("mean_var", [P, 2, CHUNK, 2])
        tab = sb("tab", [P, 8, E])
        tab_i = sb("tab_i", [P, E], I32)
        per_tile = sb("per_tile", [P, 2, E])
        per_tile2 = sb("per_tile2", [P, 2, E])
        tile_cols = sb("tile_cols", [P, 4])

        with ExitStack() as early:
            def sb1(name, shape, dt=F32):
                return sb(name, shape, dt, early)

            w_rows = [sb1(f"w_rows{i}", [P, D]) for i in range(4)]
            wT_hi = [sb1(f"wT_hi{i}", [P, D], F32R) for i in range(2)]
            wT_lo = [sb1(f"wT_lo{i}", [P, D], F32R) for i in range(2)]
            wT = sb1("wT", [P, 2, D])
            woutT = sb1("woutT", [P, D])
            wvo = sb1("wvo", [P, D])
            bq = sb1("bq", [P, 1])
            bk = sb1("bk", [P, 1])
            bv = sb1("bv", [P, 1])
            bv_cols = sb1("bv_cols", [P, P])
            ones = sb1("ones", [P, P])
            bout_bc = sb1("bout_bc", [P, D])
            bvo_bc = sb1("bvo_bc", [P, D])
            wr_sb = sb1("wr_sb", [P, E])
            br_bc = sb1("br_bc", [P, E])
            iota_i = sb1("iota_i", [P, P + 1], I32)
            before = sb1("before", [P, P], BF16)
            ones_h = sb1("ones_h", [P, P], BF16)
            row_ids = sb1("row_ids", [P, 2, CHUNK])

            x_tok = [sb1(f"x_tok{i}", [P, TILES, D]) for i in range(2)]
            xT = sb1("xT", [P, S])
            xT_hi = sb1("xT_hi", [P, S], F32R)
            xT_lo = sb1("xT_lo", [P, S], F32R)
            qkT_hi = [[sb1(f"{n}T_hi{i}", [P, S], F32R) for n in "qk"] for i in range(2)]
            qkT_lo = [[sb1(f"{n}T_lo{i}", [P, S], F32R) for n in "qk"] for i in range(2)]
            v_sum = sb1("v_sum", [P, CHUNK, D])
            v_hi = [sb1(f"v_hi{i}", [P, KT, D], F32R) for i in range(2)]
            v_lo = [sb1(f"v_lo{i}", [P, KT, D], F32R) for i in range(2)]
            minus_max = sb1("minus_max", [P, 2])
            probs = [sb1(f"probs{i}", [P, S]) for i in range(2)]
            total = sb1("total", [P, 2 * TILES])
            inv_total = sb1("inv_total", [P, CHUNK])
            pT_hi = [sb1(f"pT_hi{i}", [P, KT, CW], F32R) for i in range(2)]
            pT_lo = [sb1(f"pT_lo{i}", [P, KT, CW], F32R) for i in range(2)]
            attnT = sb1("attnT", [P, CW])
            x_res = [sb1(f"x_res{i}", [P, CHUNK, D]) for i in range(2)]
            summed = sb1("summed", [P, CHUNK, D])
            x1 = [sb1(f"x1_{i}", [P, CHUNK, ROW]) for i in range(2)]
            x1T = sb1("x1T", [P, CW])
            logits = sb1("logits", [P, CHUNK, E])
            top = sb1("top", [P, CHUNK, 8])
            top_i = sb1("top_i", [P, CHUNK, 8], U32)
            top_f = sb1("top_f", [P, CHUNK, 2])
            picked = sb1("picked", [P, 2, CHUNK, E])
            picked_h = sb1("picked_h", [P, CHUNK, E], BF16)
            shifted = sb1("shifted", [P, CHUNK, E + 2])
            expd = sb1("expd", [P, CHUNK, E + 2])
            gate_sum = sb1("gate_sum", [P, 4, CHUNK])
            gate_p = sb1("gate_p", [P, CHUNK, 2])
            rank = sb1("rank", [P, CHUNK, E])
            rank_k = sb1("rank_k", [P, 2, CHUNK, E])
            place_f = sb1("place_f", [P, 2, CHUNK])
            place = [sb1(f"place{i}", [P, 2, CHUNK], U32) for i in range(2)]

        def sb2(name, shape, dt=F32):
            return sb(name, shape, dt, late)

        row_in = [sb2(f"row_in{i}", [P, CHUNK, ROW]) for i in range(2)]
        inT = [sb2(f"inT{i}", [P, CW]) for i in range(2)]
        hidden = [sb2(f"hidden{i}", [P, CHUNK, H]) for i in range(2)]
        normed = [sb2(f"normed{i}", [P, CHUNK, H]) for i in range(2)]
        actT = [sb2(f"actT{i}", [P, CW]) for i in range(2)]
        row_out = [sb2(f"row_out{i}", [P, CHUNK, D]) for i in range(2)]
        dest_f = [sb2(f"dest_f{i}", [P, CHUNK]) for i in range(2)]
        dest = [sb2(f"dest{i}", [P, CHUNK], U32) for i in range(2)]
        pair = [sb2(f"pair{i}", [P, CHUNK, 2 * D]) for i in range(2)]
        resid = [sb2(f"resid{i}", [P, CHUNK, D]) for i in range(2)]
        mixed = [sb2(f"mixed{i}", [P, CHUNK, D]) for i in range(2)]
        shift = sb2("shift", [P, 2, CHUNK])
        minus_mean = sb2("minus_mean", [P, 2, CHUNK])
        final = [sb2(f"final{i}", [P, CHUNK, D]) for i in range(2)]

        scores = [ctx.enter_context(nc.psum_tensor(f"scores{i}", [P, 2, 512], F32)) for i in range(2)]
        turned = ctx.enter_context(nc.psum_tensor("turned", [P, 2, 512], F32))
        value_sum = ctx.enter_context(nc.psum_tensor("value_sum", [P, 512], F32))
        work = ctx.enter_context(nc.psum_tensor("work", [P, 512], F32))

        (weights_in, consts_in, expert_in, iota_done, ident_ready, setup_pe, setup_dve,
         proj_filled, proj_split, proj_taken, scores_ready, max_ready, probs_ready, turned_ready,
         pT_hi_ready, pT_lo_ready, values_ready, attnT_copied, attn_ready, attn_taken,
         var_ready, rstd_ready, x1_ready, x1_turned, x1T_ready, logits_ready, logits_taken,
         mask_ready, exp_ready, rank_ready, rank_taken, place_ready, pad_ready, pad_in,
         table_pe, table_ready, pool_const, v_ready, cols_ready) = [sem(n) for n in (
             "weights_in consts_in expert_in iota_done ident_ready setup_pe setup_dve "
             "proj_filled proj_split proj_taken scores_ready max_ready probs_ready turned_ready "
             "pT_hi_ready pT_lo_ready values_ready attnT_copied attn_ready attn_taken "
             "var_ready rstd_ready x1_ready x1_turned x1T_ready logits_ready logits_taken "
             "mask_ready exp_ready rank_ready rank_taken place_ready pad_ready pad_in "
             "table_pe table_ready pool_const v_ready cols_ready").split()]
        x_in = [sem(f"x_in{i}") for i in range(2)]
        res_in = [sem(f"res_in{i}") for i in range(2)]
        scattered = [sem(f"scattered{i}") for i in range(2)]
        kept_out = [sem(f"kept_out{i}") for i in range(2)]
        rows_in = [sem(f"rows_in{i}") for i in range(2)]
        (in_turned, inT_ready, hidden_ready, ev_ready, er_ready, normed_ready, norm_turned,
         actT_ready, result_ready) = [sem(n) for n in (
             "in_turned inT_ready hidden_ready ev_ready er_ready normed_ready norm_turned "
             "actT_ready result_ready").split()]
        result_taken = [sem(f"result_taken{i}") for i in range(2)]
        delivered = [sem(f"delivered{i}") for i in range(2)]
        pair_in = [sem(f"pair_in{i}") for i in range(2)]
        fv_ready, fr_ready = sem("fv_ready"), sem("fr_ready")
        final_ready = [sem(f"final_ready{i}") for i in range(2)]
        final_out = [sem(f"final_out{i}") for i in range(2)]
        dve_chain, dve_held, pool_held = sem("dve_chain"), sem("dve_held"), sem("pool_held")

        BATCH_LOOPS = (NB - 2) // 2
        block = ctx.enter_context(nc.Block())

        @block.sync
        def _(sp):
            sp.dma_start(x_tok[0][:], x_v[0]).then_inc(x_in[0], 16)
            for i, w in enumerate((w_q, w_k, w_v, w_out)):
                sp.dma_start(w_rows[i][:], w).then_inc(weights_in, 16)
            for dst, b in ((bq, b_q), (bk, b_k), (bv, b_v)):
                sp.dma_start(dst[:], b.rearrange("(d a) -> d a", a=1)).then_inc(consts_in, 16)
            sp.dma_start(bout_bc[:], b_out.rearrange("(a d) -> a d", a=1).to_broadcast([P, D])).then_inc(consts_in, 16)
            sp.dma_start(wr_sb[:], w_r).then_inc(consts_in, 16)
            sp.dma_start(br_bc[:], b_r.rearrange("(a d) -> a d", a=1).to_broadcast([P, E])).then_inc(consts_in, 16)
            sp.dma_start(x_tok[1][:], x_v[1]).then_inc(x_in[1], 16)
            sp.dma_start(g_rows[:, 0, :], g_1).then_inc(expert_in, 16)
            sp.dma_start(g_rows[:, 1, :], be_1).then_inc(expert_in, 16)
            sp.dma_start(w1_sb[:], w_1.rearrange("e i h -> i e h")).then_inc(expert_in, 16)
            sp.dma_start(w2_sb[:], w_2.rearrange("e i h -> i e h")).then_inc(expert_in, 16)
            sp.dma_start(b1_bc[:], b_1.rearrange("(a e) h -> a e h", a=1).to_broadcast([P, E, H])).then_inc(expert_in, 16)
            sp.dma_start(b2_bc[:], b_2.rearrange("(a e) h -> a e h", a=1).to_broadcast([P, E, D])).then_inc(expert_in, 16)

            def batch(n, m, p, first=False, load=True, keep=True):
                for c in range(2):
                    wait(sp, attn_taken, 2 * n + c - 1)
                    sp.dma_start(x_res[c][:], x_v[n][:, CHUNK * c:CHUNK * (c + 1), :]).then_inc(res_in[c], 16)
                    if keep:
                        wait(sp, x1_ready, 2 * n + c - 1)
                        sp.dma_start(kept_v[n - 1][c], x1[c][:, :, 0:D]).then_inc(kept_out[c], 16)
                if load:
                    wait(sp, proj_filled, 8 * n + 2)
                    sp.dma_start(x_tok[p][:], x_v[n + 2]).then_inc(x_in[p], 16)

            batch(0, 0, 0, keep=False)
            with sp.Fori(0, BATCH_LOOPS - 1) as i:
                batch(2 * i + 1, i, 1)
                batch(2 * i + 2, i + 1, 0)
            batch(NB - 3, 0, 1)
            batch(NB - 2, 0, 0, load=False)
            batch(NB - 1, 0, 1, load=False)
            for c in range(2):
                wait(sp, x1_ready, 2 * NB + c - 1)
                sp.dma_start(kept_v[NB - 1][c], x1[c][:, :, 0:D]).then_inc(kept_out[c], 16)

            sp.wait_ge(pad_ready, 1)
            for e in range(E):
                start = sp.value_load(base_i[0:1, e:e + 1], min_val=e * REGION, max_val=e * REGION + N)
                sp.dma_start(routed[bass.ds(start, P), :], pad_row[:]).then_inc(pad_in, 16)
            sp.wait_ge(pad_in, 16 * E)
            for c in range(2):
                sp.wait_ge(scattered[c], 16 * 2 * CHUNK * (CHUNKS // 2))
                sp.wait_ge(kept_out[c], 16 * NB)
            sp.wait_ge(table_ready, 1)

            def rows(g, m, p):
                wait(sp, in_turned, g - 1)
                wait(sp, ev_ready, g - 1)
                for t in range(CHUNK):
                    row = sp.value_load(tile_table[0:1, bass.ds(g * CHUNK + 2 * P + t, 1)],
                                        min_val=0, max_val=E * REGION - P)
                    sp.dma_start(row_in[p][:, t, :], routed[bass.ds(row, P), :]).then_inc(rows_in[p], 16)

            rows(0, 0, 0)
            rows(1, 0, 1)
            with sp.Fori(0, GROUPS // 2 - 1) as i:
                rows(2 * i + 2, i + 1, 0)
                rows(2 * i + 3, i + 1, 1)

            for p in range(2):
                sp.wait_ge(delivered[p], 16 * CHUNK * (GROUPS // 2))

            def mix_in(n, c):
                sp.dma_start(pair[c][:], chosen_v[n][c]).then_inc(pair_in[c], 16)
                sp.dma_start(resid[c][:], kept_v[n][c]).then_inc(pair_in[c], 16)

            mix_in(0, 0)
            mix_in(0, 1)
            with sp.Fori(0, NB - 1) as n:
                for c in range(2):
                    sp.wait_ge(final_ready[c], n + 1)
                    sp.dma_start(out_v[n][c], final[c][:]).then_inc(final_out[c], 16)
                    mix_in(n + 1, c)
            for c in range(2):
                sp.wait_ge(final_ready[c], NB)
                sp.dma_start(out_v[NB - 1][c], final[c][:]).then_inc(final_out[c], 16)
            for c in range(2):
                sp.wait_ge(final_out[c], 16 * NB)

        @block.gpsimd
        def _(pool):
            def hold():
                pool.sem_inc(pool_held, 1)

            pool.iota(iota_i[:, 0:P], [[1, P]], base=0, channel_multiplier=0).then_inc(iota_done, 1)
            pool.iota(iota_i[:, P:P + 1], [[1, 1]], base=0, channel_multiplier=1).then_inc(iota_done, 1)
            pool.memset(minus_half[:], -0.5).then_inc(pool_const, 1)
            pool.memset(ones_h[:], 1.0).then_inc(pool_const, 1)
            pool.memset(pad_row[:], 0.0).then_inc(pool_const, 1)
            pool.memset(x1[0][:], 0.0).then_inc(pool_const, 1)
            pool.memset(x1[1][:], 0.0).then_inc(pool_const, 1)
            pool.wait_ge(pool_const, 5)

            def scale_and_scatter(C, c, k):
                pool.wait_ge(var_ready, C + 1)
                pool.tensor_tensor(rstd[:, 0, :], var[:, 0, :], minus_half[:], ALU.pow).then_inc(rstd_ready, 1)
                pool.wait_ge(place_ready, C + 1)
                hold()
                for t in range(CHUNK):
                    for s in range(2):
                        pool.indirect_dma_start(
                            routed, bass.IndirectOffsetOnAxis(ap=place[c][:, s, t:t + 1], axis=0),
                            x1[c][:, t, :], None).then_inc(scattered[c], 16)

            with pool.Fori(0, CHUNKS // 2) as i:
                for c in range(2):
                    scale_and_scatter(2 * i + c, c, i)

            def expert_group(g, p):
                pool.wait_ge(ev_ready, g + 1)
                pool.tensor_tensor(rstd[:, p, :], var[:, p, :], minus_half[:], ALU.pow).then_inc(er_ready, 1)

            def deliver(m, p):
                pool.wait_ge(result_taken[p], m + 1)
                hold()
                for t in range(CHUNK):
                    pool.indirect_dma_start(
                        chosen, bass.IndirectOffsetOnAxis(ap=dest[p][:, t:t + 1], axis=0),
                        row_out[p][:, t, :], None, bounds_check=2 * N - 1,
                        oob_is_err=False).then_inc(delivered[p], 16)

            expert_group(0, 0)
            with pool.Fori(0, GROUPS // 2 - 1) as i:
                expert_group(2 * i + 1, 1)
                deliver(i, 0)
                expert_group(2 * i + 2, 0)
                deliver(i, 1)
            expert_group(GROUPS - 1, 1)
            deliver(GROUPS // 2 - 1, 0)
            deliver(GROUPS // 2 - 1, 1)

            with pool.Fori(0, NB) as n:
                for c in range(2):
                    pool.wait_ge(fv_ready, 2 * n + c + 1)
                    pool.tensor_tensor(rstd[:, c, :], var[:, c, :], minus_half[:], ALU.pow).then_inc(fr_ready, 1)
                    pool.wait_ge(fr_ready, 4 * n + 2 * c + 1)
                    pool.tensor_tensor(shift[:, c, :], minus_mean[:, c, :], rstd[:, c, :],
                                       ALU.mult).then_inc(fr_ready, 1)

        @block.tensor
        def _(pe):
            pe.wait_ge(weights_in, 64)
            pe.wait_ge(ident_ready, 1)
            for i, src in enumerate((0, 1, 3)):
                mm = pe.transpose(work[:, i * P:(i + 1) * P], w_rows[src][:], ident[:])
            mm.then_inc(setup_pe, 1)
            pe.wait_ge(setup_dve, 2)
            pe.matmul(value_sum[:, 0:D], w_rows[2][:], woutT[:], start=True, stop=True)
            pe.matmul(value_sum[:, D:2 * D], bv_cols[:], woutT[:], start=True, stop=True)
            pe.wait_ge(expert_in, 96)
            for i in range(2):
                mm = pe.transpose(value_sum[:, 2 * D + i * E:2 * D + (i + 1) * E], g_rows[:, i, :], ident[0:E, 0:E])
            mm.then_inc(setup_pe, 1)
            pe.wait_ge(setup_dve, 5)

            def three_passes(dst, a_hi, a_lo, b_hi, b_lo, start=True, stop=True):
                pe.matmul(dst, a_hi, b_hi, start=start, stop=False)
                pe.matmul(dst, a_hi, b_lo, start=False, stop=False)
                return pe.matmul(dst, a_lo, b_hi, start=False, stop=stop)

            def project(n, m, p, j):
                h = j % 2
                cols = slice(h * CW, (h + 1) * CW)
                if j < 2:
                    pe.wait_ge(x_in[p], 16 * (m + 1))
                    for t in range(CHUNK):
                        mm = pe.transpose(work[:, t * P:(t + 1) * P], x_tok[p][:, h * CHUNK + t, :], ident[:])
                elif j < 6:
                    k = (j - 2) // 2
                    pe.wait_ge(proj_taken, 8 * n + 2)
                    mm = three_passes(work[:], wT_hi[k][:], wT_lo[k][:], xT_hi[:, cols], xT_lo[:, cols])
                else:
                    for t in range(CHUNK):
                        mm = pe.matmul(work[:, t * D:(t + 1) * D],
                                       xT[:, h * CW + t * P:h * CW + (t + 1) * P], wvo[:], start=True, stop=True)
                mm.then_inc(proj_filled, 1)

            def score(s, p, j):
                wait(pe, probs_ready, s - 1)
                q = slice(j * P, (j + 1) * P)
                for h in range(2):
                    k = slice(h * CW, (h + 1) * CW)
                    mm = three_passes(scores[j % 2][:, h, :], qkT_hi[p][0][:, q], qkT_lo[p][0][:, q],
                                      qkT_hi[p][1][:, k], qkT_lo[p][1][:, k])
                mm.then_inc(scores_ready, 1)

            def turn(s, j):
                pe.wait_ge(probs_ready, s + 1)
                for h in range(2):
                    wait(pe, pT_lo_ready, 2 * (s - 1) + h + 1)
                    for t in range(4):
                        k = 4 * h + t
                        mm = pe.transpose(turned[:, h, t * P:(t + 1) * P],
                                          probs[j % 2][:, k * P:(k + 1) * P], ident[:])
                    mm.then_inc(turned_ready, 1)

            def weigh(C, c, vp, r):
                if r == 0:
                    pe.wait_ge(pT_lo_ready, 8 * (C + 1))
                    wait(pe, attnT_copied, C)
                for k in (2 * r, 2 * r + 1):
                    mm = three_passes(value_sum[:], v_hi[vp][:, k, :], v_lo[vp][:, k, :],
                                      pT_hi[c][:, k, :], pT_lo[c][:, k, :], start=(k == 0), stop=(k == KT - 1))
                if r == 3:
                    mm.then_inc(values_ready, 1)

            def route(C, c, r):
                if r == 0:
                    pe.wait_ge(attnT_copied, C + 1)
                    for t in range(CHUNK):
                        mm = pe.transpose(work[:, t * P:(t + 1) * P], attnT[:, t * P:(t + 1) * P], ident[:])
                    mm.then_inc(attn_ready, 1)
                elif r == 1:
                    pe.wait_ge(x1_ready, C + 1)
                    for t in range(CHUNK):
                        mm = pe.transpose(work[:, t * P:(t + 1) * P], x1[c][:, t, 0:D], ident[:])
                    mm.then_inc(x1_turned, 1)
                elif r == 2:
                    pe.wait_ge(x1T_ready, C + 1)
                    for t in range(CHUNK):
                        mm = pe.matmul(work[:, t * E:(t + 1) * E], x1T[:, t * P:(t + 1) * P], wr_sb[:],
                                       start=True, stop=True)
                    mm.then_inc(logits_ready, 1)
                else:
                    pe.wait_ge(mask_ready, C + 1)
                    mask = picked_h[:].rearrange("p t e -> p (t e)")
                    pe.matmul(work[:, 0:CHUNK * E], before[:], mask, start=True, stop=True)
                    pe.matmul(work[:, CHUNK * E:2 * CHUNK * E], ones_h[:], mask, start=True, stop=True)\
                        .then_inc(rank_ready, 1)

            def work_free(C, r):
                seen = (rank_taken, attn_taken, x1T_ready, logits_taken)[r]
                wait(pe, seen, C if r == 0 else C + 1)

            def batch(n, m, p, score_next=True, project_next=True):
                for j in range(TILES):
                    c, r = j // CHUNK, j % CHUNK
                    s, C = TILES * n + j, 2 * n + c
                    if project_next:
                        if j == 0 or (isinstance(n, int) and n == 0):
                            pe.wait_ge(proj_taken, 8 * (n + 1) + j)
                        work_free(C - 2, r)
                        project(n + 1, m + p, 1 - p, j)
                    if j < TILES - 1:
                        score(s + 1, p, j + 1)
                    elif score_next:
                        pe.wait_ge(proj_taken, 8 * (n + 1) + 6)
                        score(s + 1, 1 - p, 0)
                    if not (isinstance(n, int) and n == 0 and c == 0):
                        if r == 0 and c == 0:
                            pe.wait_ge(v_ready, 2 * n)
                        if r == 0 and c == 1:
                            pe.wait_ge(v_ready, 2 * n + 2)
                        weigh(C - 1, 1 - c, (1 - p) if c == 0 else p, r)
                    if not (isinstance(n, int) and n == 0):
                        if project_next:
                            pe.wait_ge(proj_taken, 8 * (n + 1) + j + 1)
                        else:
                            work_free(C - 2, r)
                        route(C - 2, c, r)
                    turn(s, j)

            for j in range(TILES):
                if j:
                    pe.wait_ge(proj_taken, j)
                project(0, 0, 0, j)
            pe.wait_ge(proj_taken, 8)
            score(0, 0, 0)
            batch(0, 0, 0)
            with pe.Fori(0, BATCH_LOOPS) as i:
                batch(2 * i + 1, i, 1)
                batch(2 * i + 2, i + 1, 0)
            batch(NB - 1, NB // 2 - 1, 1, score_next=False, project_next=False)
            for c in range(2):
                C = CHUNKS + c
                for r in range(4):
                    if c == 0:
                        weigh(C - 1, 1, 1, r)
                    work_free(C - 2, r)
                    route(C - 2, c, r)

            pe.wait_ge(cols_ready, 2)
            for i in range(4):
                mm = pe.matmul(work[0:1, i * P:(i + 1) * P], tile_cols[:, i:i + 1], ident[:], start=True, stop=True)
            mm.then_inc(table_pe, 1)
            pe.wait_ge(table_ready, 1)

            def experts_of(g):
                return [pe.value_load(tile_table[0:1, bass.ds(g * CHUNK + t, 1)], min_val=0, max_val=E - 1)
                        for t in range(CHUNK)]

            def turn_rows(g, m, p):
                pe.wait_ge(rows_in[p], 16 * CHUNK * (m + 1))
                wait(pe, inT_ready, g - 1)
                for t in range(CHUNK):
                    mm = pe.transpose(scores[p][:, 0, t * P:(t + 1) * P], row_in[p][:, t, 0:D], ident[:])
                mm.then_inc(in_turned, 1)

            def first_product(g, p, experts):
                pe.wait_ge(inT_ready, g + 1)
                wait(pe, ev_ready, g - 1)
                for t in range(CHUNK):
                    mm = pe.matmul(scores[p][:, 1, t * H:(t + 1) * H], inT[p][:, t * P:(t + 1) * P],
                                   w1_sb[:, bass.ds(experts[t], 1), :], start=True, stop=True)
                mm.then_inc(hidden_ready, 1)

            def turn_hidden(g, p):
                pe.wait_ge(normed_ready, g + 1)
                for t in range(CHUNK):
                    mm = pe.transpose(turned[:, p, t * P:(t + 1) * P], normed[p][:, t, :], ident[:])
                mm.then_inc(norm_turned, 1)

            def second_product(g, m, p, experts):
                pe.wait_ge(actT_ready, g + 1)
                pe.wait_ge(result_taken[p], m)
                dst = (value_sum, work)[p]
                for t in range(CHUNK):
                    mm = pe.matmul(dst[:, t * D:(t + 1) * D], actT[p][:, t * P:(t + 1) * P],
                                   w2_sb[:, bass.ds(experts[t], 1), :], start=True, stop=True)
                mm.then_inc(result_ready, 1)

            def step(g, m, p, first=False, last=False):
                if not last:
                    turn_rows(g, m, p)
                if not first:
                    turn_hidden(g - 1, 1 - p)
                if not last:
                    first_product(g, p, experts_of(g))
                if not first:
                    second_product(g - 1, m - 1 + p, 1 - p, experts_of(g - 1))

            step(0, 0, 0, first=True)
            with pe.Fori(0, GROUPS // 2 - 1) as i:
                step(2 * i + 1, i, 1)
                step(2 * i + 2, i + 1, 0)
            step(GROUPS - 1, GROUPS // 2 - 1, 1)
            step(GROUPS, GROUPS // 2, 0, last=True)

        @block.scalar
        def _(act):
            act.preload_act_table(ACT.Exp)
            act.wait_ge(setup_dve, 5)

            def project(n, p, j):
                h = j % 2
                cols = slice(h * CW, (h + 1) * CW)
                if j < 6:
                    act.wait_ge(proj_filled, 8 * n + j + 1)
                if j < 2:
                    act.copy(xT[:, cols], work[:])
                    act.copy(xT_hi[:, cols], work[:]).then_inc(proj_split, 1)
                elif j < 6:
                    k = (j - 2) // 2
                    act.activation(qkT_hi[p][k][:, cols], work[:], ACT.Identity,
                                   bias=(bq, bk)[k][:, 0:1]).then_inc(proj_split, 1)
                else:
                    act.wait_ge(proj_taken, 8 * n + j + 1)
                    wait(act, values_ready, 2 * (n - 2) + 2)
                    act.copy(v_hi[p][:, h * CHUNK:(h + 1) * CHUNK, :], v_sum[:]).then_inc(proj_split, 1)

            def exponent(s, j, zp):
                act.wait_ge(max_ready, s + 1)
                wait(act, turned_ready, 2 * (s - 1))
                act.activation(probs[j % 2][:], scores[j % 2][:].rearrange("p a b -> p (a b)"), ACT.Exp,
                               bias=minus_max[:, j % 2:j % 2 + 1],
                               accum_out=total[:, zp * TILES + j:zp * TILES + j + 1]).then_inc(probs_ready, 1)

            def high(s, C, c, r):
                if r == 0:
                    wait(act, values_ready, C - 1)
                for h in range(2):
                    act.wait_ge(turned_ready, 2 * s + h + 1)
                    act.copy(pT_hi[c][:, 4 * h:4 * h + 4, r * P:(r + 1) * P],
                             turned[:, h, :].rearrange("p (k q) -> p k q", k=4)).then_inc(pT_hi_ready, 1)

            def copy_values(C):
                act.wait_ge(values_ready, C + 1)
                wait(act, attn_ready, C)
                act.copy(attnT[:], value_sum[:]).then_inc(attnT_copied, 1)

            def route(C, r):
                if r == 1:
                    act.wait_ge(x1_turned, C + 1)
                    wait(act, logits_ready, C)
                    act.copy(x1T[:], work[:]).then_inc(x1T_ready, 1)
                if r == 3:
                    act.wait_ge(mask_ready, C + 1)
                    act.activation(expd[:], shifted[:], ACT.Exp).then_inc(exp_ready, 1)

            def batch(n, p, score_next=True, project_next=True):
                for j in range(TILES):
                    c, r = j // CHUNK, j % CHUNK
                    s, C = TILES * n + j, 2 * n + c
                    if project_next:
                        project(n + 1, 1 - p, j)
                    if j < TILES - 1:
                        exponent(s + 1, j + 1, p)
                    elif score_next:
                        exponent(s + 1, 0, 1 - p)
                    if r == 3 and not (isinstance(n, int) and n == 0 and c == 0):
                        copy_values(C - 1)
                    if not (isinstance(n, int) and n == 0):
                        route(C - 2, r)
                    high(s, C, c, r)

            for j in range(TILES):
                project(0, 0, j)
            exponent(0, 0, 0)
            batch(0, 0)
            with act.Fori(0, BATCH_LOOPS) as i:
                batch(2 * i + 1, 1)
                batch(2 * i + 2, 0)
            batch(NB - 1, 1, score_next=False, project_next=False)
            for c in range(2):
                C = CHUNKS + c
                for r in range(4):
                    if r == 3 and c == 0:
                        copy_values(C - 1)
                    route(C - 2, r)

            act.preload_act_table(ACT.Gelu)
            act.wait_ge(table_ready, 1)

            def take_rows(g, p):
                act.wait_ge(in_turned, g + 1)
                wait(act, hidden_ready, g - 1)
                act.copy(inT[p][:], scores[p][:, 0, :]).then_inc(inT_ready, 1)

            def gelu(g, p):
                experts = [act.value_load(tile_table[0:1, bass.ds(g * CHUNK + t, 1)], min_val=0, max_val=E - 1)
                           for t in range(CHUNK)]
                act.wait_ge(norm_turned, g + 1)
                for t in range(CHUNK):
                    a = act.activation(actT[p][:, t * P:(t + 1) * P], turned[:, p, t * P:(t + 1) * P], ACT.Gelu,
                                       bias=g_cols[:, 1, bass.ds(experts[t], 1)],
                                       scale=g_cols[:, 0, bass.ds(experts[t], 1)])
                a.then_inc(actT_ready, 1)

            take_rows(0, 0)
            with act.Fori(0, GROUPS // 2 - 1) as i:
                take_rows(2 * i + 1, 1)
                gelu(2 * i, 0)
                take_rows(2 * i + 2, 0)
                gelu(2 * i + 1, 1)
            take_rows(GROUPS - 1, 1)
            gelu(GROUPS - 2, 0)
            gelu(GROUPS - 1, 1)

            with act.Fori(0, NB) as n:
                for c in range(2):
                    act.wait_ge(fr_ready, 4 * n + 2 * c + 2)
                    act.wait_ge(final_out[c], 16 * n)
                    for t in range(CHUNK):
                        a = act.activation(final[c][:, t, :], mixed[c][:, t, :], ACT.Identity,
                                           bias=shift[:, c, t:t + 1], scale=rstd[:, c, t:t + 1])
                    a.then_inc(final_ready[c], 1)

        @block.vector
        def _(dve):
            chain = Chain(dve, dve_chain)
            then, sync = chain.then, chain.sync

            def hold():
                dve.sem_inc(dve_held, 1)


            dve.wait_ge(iota_done, 2)
            then(dve.tensor_copy(column[:], iota_i[:, 0:P]))
            then(dve.tensor_copy(partition[:], iota_i[:, P:P + 1]))
            then(dve.tensor_copy(expert_ids[:], iota_i[:, 0:E]))
            sync()
            dve.tensor_scalar(ident[:], column[:], partition[:, 0:1], None, ALU.is_equal).then_inc(ident_ready, 1)
            then(dve.tensor_scalar(before[:], column[:], partition[:, 0:1], None, ALU.is_gt))
            then(dve.memset(ones[:], 1.0))
            then(dve.tensor_scalar(region_start[:], expert_ids[:], float(REGION), None, ALU.mult))
            sync()
            then(dve.tensor_copy(base[:, CHUNK, :], region_start[:]))
            for c in range(2):
                for t in range(CHUNK):
                    then(dve.tensor_scalar(row_ids[:, c, t:t + 1], partition[:], 2.0 * TILES,
                                           2.0 * (CHUNK * c + t), ALU.mult, ALU.add))
            dve.wait_ge(pool_const, 5)
            then(dve.memset(pad_row[:, D:D + 1], 2.0 * N))
            then(dve.memset(pad_row[:, D + 1:D + 2], -1.0))
            dve.wait_ge(consts_in, 96)
            then(dve.tensor_scalar(bq[:], bq[:], SCALE, None, ALU.mult))
            then(dve.tensor_scalar(bv_cols[:], ones[:], bv[:, 0:1], None, ALU.mult))
            dve.wait_ge(setup_pe, 1)
            then(dve.tensor_scalar(wT[:, 0, :], work[:, 0:D], SCALE, None, ALU.mult))
            then(dve.tensor_copy(wT[:, 1, :], work[:, D:2 * D]))
            then(dve.tensor_copy(woutT[:], work[:, 2 * D:3 * D]))
            sync()
            for i in range(2):
                then(dve.tensor_copy(wT_hi[i][:], wT[:, i, :]))
            sync()
            for i in range(2):
                dve.tensor_tensor(wT_lo[i][:], wT[:, i, :], wT_hi[i][:].bitcast(F32),
                                  ALU.subtract).then_inc(setup_dve, 1)
            dve.wait_ge(setup_pe, 2)
            dve.tensor_copy(wvo[:], value_sum[:, 0:D]).then_inc(setup_dve, 1)
            dve.tensor_tensor(bvo_bc[:], value_sum[:, D:2 * D], bout_bc[:], ALU.add).then_inc(setup_dve, 1)
            dve.tensor_copy(g_cols[:], value_sum[:, 2 * D:2 * D + 2 * E].rearrange("p (a e) -> p a e", a=2))\
                .then_inc(setup_dve, 1)
            dve.wait_ge(setup_dve, 5)

            def project(n, p, j):
                h = j % 2
                cols = slice(h * CW, (h + 1) * CW)
                if j < 2:
                    dve.wait_ge(proj_split, 8 * n + j + 1)
                    dve.tensor_tensor(xT_lo[:, cols], work[:], xT_hi[:, cols].bitcast(F32),
                                      ALU.subtract).then_inc(proj_taken, 1)
                elif j < 6:
                    k = (j - 2) // 2
                    dve.wait_ge(proj_split, 8 * n + j + 1)
                    dve.scalar_tensor_tensor(out=qkT_lo[p][k][:, cols], in0=work[:], scalar=(bq, bk)[k][:, 0:1],
                                             in1=qkT_hi[p][k][:, cols].bitcast(F32), op0=ALU.add,
                                             op1=ALU.subtract).then_inc(proj_taken, 1)
                else:
                    dve.wait_ge(proj_filled, 8 * n + j + 1)
                    wait(dve, v_ready, 2 * n + h)
                    dve.tensor_tensor(v_sum[:], work[:].rearrange("p (t d) -> p t d", t=CHUNK),
                                      bvo_bc[:].rearrange("p (a d) -> p a d", a=1).to_broadcast([P, CHUNK, D]),
                                      ALU.add).then_inc(proj_taken, 1)

            def low_values(n, p, j):
                h = j % 2
                dve.wait_ge(proj_split, 8 * n + j + 1)
                wait(dve, values_ready, 2 * (n - 2) + 2)
                part = slice(h * CHUNK, (h + 1) * CHUNK)
                dve.tensor_tensor(v_lo[p][:, part, :], v_sum[:], v_hi[p][:, part, :].bitcast(F32),
                                  ALU.subtract).then_inc(v_ready, 1)

            def maximum(s, j):
                dve.wait_ge(scores_ready, s + 1)
                dve.tensor_reduce(minus_max[:, j % 2:j % 2 + 1], scores[j % 2][:], AX.XY, ALU.max,
                                  negate=True).then_inc(max_ready, 1)

            def low(s, C, c, r):
                if r == 0:
                    wait(dve, values_ready, C - 1)
                for h in range(2):
                    dve.wait_ge(pT_hi_ready, 2 * s + h + 1)
                    part = pT_hi[c][:, 4 * h:4 * h + 4, r * P:(r + 1) * P]
                    dve.tensor_tensor(pT_lo[c][:, 4 * h:4 * h + 4, r * P:(r + 1) * P],
                                      turned[:, h, :].rearrange("p (k q) -> p k q", k=4), part.bitcast(F32),
                                      ALU.subtract).then_inc(pT_lo_ready, 1)

            def route_early(C, c, r, zp, k):
                if r == 0:
                    z = zp * TILES + c * CHUNK
                    then(dve.reciprocal(inv_total[:], total[:, z:z + CHUNK]))
                    sync()
                    dve.wait_ge(attn_ready, C + 1)
                    dve.wait_ge(res_in[c], 16 * (k + 1))
                    for t in range(CHUNK):
                        a = dve.scalar_tensor_tensor(out=summed[:, t, :], in0=work[:, t * P:(t + 1) * P],
                                                     scalar=inv_total[:, t:t + 1], in1=x_res[c][:, t, :],
                                                     op0=ALU.mult, op1=ALU.add)
                        if t == CHUNK - 1:
                            a.then_inc(attn_taken, 1)
                    dve.wait_ge(attn_taken, C + 1)
                    for t in range(CHUNK):
                        then(dve.bn_stats(stats[:, 0, t, :], summed[:, t, :]))
                    sync()
                    hold()
                    for t in range(CHUNK):
                        then(dve.bn_aggr(mean_var[:, 0, t, :], stats[:, 0, t, :]))
                    sync()
                    dve.tensor_scalar(var[:, 0, :], mean_var[:, 0, :, 1], EPS, None, ALU.add)\
                        .then_inc(var_ready, 1)
                if r == 2:
                    dve.wait_ge(logits_ready, C + 1)
                    dve.tensor_tensor(logits[:], work[:, 0:CHUNK * E].rearrange("p (t e) -> p t e", t=CHUNK),
                                      br_bc[:].rearrange("p (a e) -> p a e", a=1).to_broadcast([P, CHUNK, E]),
                                      ALU.add).then_inc(logits_taken, 1)
                    dve.wait_ge(logits_taken, C + 1)
                    hold()
                    for t in range(CHUNK):
                        then(dve.max(top[:, t, :], logits[:, t, :]))
                    sync()
                    hold()
                    for t in range(CHUNK):
                        then(dve.max_index(top_i[:, t, :], top[:, t, :], logits[:, t, :]))
                    largest = top[:, :, 0:1]
                    then(dve.tensor_tensor(shifted[:, :, 0:E], logits[:], largest.to_broadcast([P, CHUNK, E]),
                                           ALU.subtract))
                    then(dve.tensor_tensor(shifted[:, :, E:E + 2], top[:, :, 0:2],
                                           largest.to_broadcast([P, CHUNK, 2]), ALU.subtract))
                    sync()
                    then(dve.tensor_copy(top_f[:], top_i[:, :, 0:2]))
                    sync()
                    ids = expert_ids[:].rearrange("p (a e) -> p a e", a=1).to_broadcast([P, CHUNK, E])
                    for s in range(2):
                        then(dve.tensor_tensor(picked[:, s], ids, top_f[:, :, s:s + 1].to_broadcast([P, CHUNK, E]),
                                               ALU.is_equal))
                    sync()
                    dve.tensor_tensor(picked_h[:], picked[:, 0], picked[:, 1], ALU.add).then_inc(mask_ready, 1)
                if r == 3:
                    dve.wait_ge(rank_ready, C + 1)
                    then(dve.tensor_copy(base[:, 0, :], base[:, CHUNK, :]))
                    for t in range(CHUNK):
                        sync()
                        col = (CHUNK + t) * E
                        then(dve.tensor_tensor(base[:, t + 1, :], base[:, t, :], work[:, col:col + E], ALU.add))
                    sync()
                    dve.tensor_tensor(rank[:], work[:, 0:CHUNK * E].rearrange("p (t e) -> p t e", t=CHUNK),
                                      base[:, 0:CHUNK, :], ALU.add).then_inc(rank_taken, 1)
                    dve.wait_ge(rank_taken, C + 1)
                    for s in range(2):
                        then(dve.tensor_tensor(rank_k[:, s], picked[:, s], rank[:], ALU.mult))
                    then(dve.tensor_copy(x1[c][:, :, D:D + 1], row_ids[:, c, :].rearrange("p (t a) -> p t a", a=1)))
                    then(dve.tensor_copy(x1[c][:, :, D + 1:D + 2], top_f[:, :, 1:2]))
                    sync()
                    then(dve.tensor_scalar(row_ids[:, c, :], row_ids[:, c, :], 2.0 * S, None, ALU.add))
                    then(dve.tensor_reduce(place_f[:], rank_k[:], AX.X, ALU.add))
                    sync()
                    dve.tensor_copy(place[c][:], place_f[:]).then_inc(place_ready, 1)
                    dve.wait_ge(exp_ready, C + 1)
                    then(dve.tensor_reduce(gate_sum[:, 0, :], expd[:, :, 0:E], AX.X, ALU.add))
                    sync()
                    then(dve.reciprocal(gate_sum[:, 1, :], gate_sum[:, 0, :]))
                    sync()
                    then(dve.tensor_tensor(gate_p[:], expd[:, :, E:E + 2],
                                           gate_sum[:, 1, :].rearrange("p (t a) -> p t a", a=1).to_broadcast([P, CHUNK, 2]),
                                           ALU.mult))
                    sync()
                    then(dve.tensor_reduce(gate_sum[:, 2, :], gate_p[:], AX.X, ALU.add))
                    sync()
                    then(dve.tensor_scalar(gate_sum[:, 2, :], gate_sum[:, 2, :], 1e-9, None, ALU.max))
                    sync()
                    then(dve.reciprocal(gate_sum[:, 3, :], gate_sum[:, 2, :]))
                    sync()
                    then(dve.tensor_tensor(gates[:, bass.ds(C, 1), :, :].rearrange("p a t k -> p (a t) k"), gate_p[:],
                                           gate_sum[:, 3, :].rearrange("p (t a) -> p t a", a=1).to_broadcast([P, CHUNK, 2]),
                                           ALU.mult))

            def normalise(C, c, k):
                dve.wait_ge(rstd_ready, C + 1)
                wait(dve, scattered[c], 16 * 2 * CHUNK * k)
                wait(dve, kept_out[c], 16 * k)
                for t in range(CHUNK):
                    a = dve.tensor_scalar(x1[c][:, t, 0:D], summed[:, t, :], mean_var[:, 0, t, 0:1],
                                          rstd[:, 0, t:t + 1], ALU.subtract, ALU.mult)
                a.then_inc(x1_ready, 1)

            def batch(n, p, score_next=True, project_next=True):
                for j in range(TILES):
                    c, r = j // CHUNK, j % CHUNK
                    s, C = TILES * n + j, 2 * n + c
                    if project_next:
                        project(n + 1, 1 - p, j)
                    if j < TILES - 1:
                        maximum(s + 1, j + 1)
                    elif score_next:
                        maximum(s + 1, 0)
                    if project_next and j >= 6:
                        low_values(n + 1, 1 - p, j)
                    if not (isinstance(n, int) and n == 0):
                        route_early(C - 2, c, r, 1 - p, n - 1)
                    low(s, C, c, r)
                    if r == 0 and not (isinstance(n, int) and n == 0):
                        normalise(C - 2, c, n - 1)

            for j in range(TILES):
                project(0, 0, j)
                if j >= 6:
                    low_values(0, 0, j)
            maximum(0, 0)
            batch(0, 0)
            per = 2 * 80
            with dve.Fori(0, BATCH_LOOPS) as i:
                chain.enter(per, i)
                batch(2 * i + 1, 1)
                batch(2 * i + 2, 0)
            chain.leave(BATCH_LOOPS)
            batch(NB - 1, 1, score_next=False, project_next=False)
            for c in range(2):
                for r in range(4):
                    route_early(CHUNKS - 2 + c, c, r, 1, NB - 1)
                    if r == 0:
                        normalise(CHUNKS - 2 + c, c, NB - 1)

            sync()
            end = base[:, CHUNK, :]
            dve.tensor_copy(base_i[:], end).then_inc(pad_ready, 1)
            count, count_i = tab[:, 0, :], tab_i
            then(dve.tensor_tensor(count, end, region_start[:], ALU.subtract))
            sync()
            then(dve.tensor_scalar(count, count, float(P - 1), None, ALU.add))
            sync()
            then(dve.tensor_copy(count_i[:], count))
            sync()
            then(dve.tensor_scalar(count_i[:], count_i[:], 7, None, ALU.logical_shift_right))
            sync()
            tiles = tab[:, 1, :]
            then(dve.tensor_copy(tiles, count_i[:]))
            upto = [tab[:, 2, :], tab[:, 3, :]]
            then(dve.tensor_copy(upto[0], count_i[:]))
            w = 1
            while w < E:
                sync()
                then(dve.tensor_tensor(upto[1][:, w:E], upto[0][:, w:E], upto[0][:, 0:E - w], ALU.add))
                then(dve.tensor_copy(upto[1][:, 0:w], upto[0][:, 0:w]))
                upto.reverse()
                w *= 2
            sync()
            for i in range(2):
                then(dve.tensor_scalar(tab[:, 4 + i, 0:1], partition[:], float(i * P), None, ALU.add))
            sync()
            for i in range(2):
                then(dve.tensor_scalar(per_tile[:, i, :], upto[0], tab[:, 4 + i, 0:1], None, ALU.is_le))
            sync()
            then(dve.tensor_tensor(per_tile2[:], per_tile[:],
                                   tiles.rearrange("p (a e) -> p a e", a=1).to_broadcast([P, 2, E]), ALU.mult))
            then(dve.tensor_reduce(tile_cols[:, 0:2], per_tile[:], AX.X, ALU.add))
            sync()
            then(dve.tensor_reduce(tab[:, 6, 0:2], per_tile2[:], AX.X, ALU.add))
            sync()
            for i in range(2):
                then(dve.tensor_tensor(tab[:, 7, i:i + 1], tab[:, 4 + i, 0:1], tab[:, 6, i:i + 1], ALU.subtract))
            sync()
            then(dve.tensor_scalar(tab[:, 7, 0:2], tab[:, 7, 0:2], float(P), None, ALU.mult))
            sync()
            then(dve.scalar_tensor_tensor(out=tab[:, 6, 0:2], in0=tile_cols[:, 0:2], scalar=float(REGION),
                                          in1=tab[:, 7, 0:2], op0=ALU.mult, op1=ALU.add))
            sync()
            dve.tensor_scalar(tile_cols[:, 2:4], tab[:, 6, 0:2], base[:, CHUNK, E - 1:E], None,
                              ALU.min).then_inc(cols_ready, 1)
            dve.tensor_scalar(tile_cols[:, 0:2], tile_cols[:, 0:2], float(E - 1), None,
                              ALU.min).then_inc(cols_ready, 1)
            dve.wait_ge(table_pe, 1)
            dve.tensor_copy(tile_table[:], work[0:1, :]).then_inc(table_ready, 1)
            dve.wait_ge(table_ready, 1)

            def hidden_rows(g, m, p):
                experts = [dve.value_load(tile_table[0:1, bass.ds(g * CHUNK + t, 1)], min_val=0, max_val=E - 1)
                           for t in range(CHUNK)]
                dve.wait_ge(hidden_ready, g + 1)
                for t in range(CHUNK):
                    then(dve.tensor_tensor(hidden[p][:, t, :], scores[p][:, 1, t * H:(t + 1) * H],
                                           b1_bc[:, bass.ds(experts[t], 1), :].rearrange("p a h -> p (a h)"), ALU.add))
                sync()
                for t in range(CHUNK):
                    then(dve.bn_stats(stats[:, p, t, :], hidden[p][:, t, :]))
                for t in range(CHUNK):
                    then(dve.scalar_tensor_tensor(
                        out=dest_f[p][:, t:t + 1], in0=expert_ids[:, bass.ds(experts[t], 1)],
                        scalar=row_in[p][:, t, D + 1:D + 2], in1=row_in[p][:, t, D:D + 1],
                        op0=ALU.is_equal, op1=ALU.add))
                sync()
                hold()
                for t in range(CHUNK):
                    then(dve.bn_aggr(mean_var[:, p, t, :], stats[:, p, t, :]))
                sync()
                dve.tensor_scalar(var[:, p, :], mean_var[:, p, :, 1], EPS, None, ALU.add).then_inc(ev_ready, 1)

            def norm_rows(g, p):
                dve.wait_ge(er_ready, g + 1)
                for t in range(CHUNK):
                    a = dve.tensor_scalar(normed[p][:, t, :], hidden[p][:, t, :], mean_var[:, p, t, 0:1],
                                          rstd[:, p, t:t + 1], ALU.subtract, ALU.mult)
                a.then_inc(normed_ready, 1)

            def results(g, m, p):
                experts = [dve.value_load(tile_table[0:1, bass.ds(g * CHUNK + t, 1)], min_val=0, max_val=E - 1)
                           for t in range(CHUNK)]
                dve.wait_ge(result_ready, g + 1)
                wait(dve, delivered[p], 16 * CHUNK * m)
                then(dve.tensor_copy(dest[p][:], dest_f[p][:]))
                sync()
                src = (value_sum, work)[p]
                for t in range(CHUNK):
                    a = dve.tensor_tensor(row_out[p][:, t, :], src[:, t * D:(t + 1) * D],
                                          b2_bc[:, bass.ds(experts[t], 1), :].rearrange("p a h -> p (a h)"), ALU.add)
                a.then_inc(result_taken[p], 1)

            hidden_rows(0, 0, 0)
            norm_rows(0, 0)
            with dve.Fori(0, GROUPS // 2 - 1) as i:
                chain.enter(8 * CHUNK + 2, i)
                hidden_rows(2 * i + 1, i, 1)
                norm_rows(2 * i + 1, 1)
                results(2 * i, i, 0)
                hidden_rows(2 * i + 2, i + 1, 0)
                norm_rows(2 * i + 2, 0)
                results(2 * i + 1, i, 1)
            chain.leave(GROUPS // 2 - 1)
            hidden_rows(GROUPS - 1, GROUPS // 2 - 1, 1)
            norm_rows(GROUPS - 1, 1)
            results(GROUPS - 2, GROUPS // 2 - 1, 0)
            results(GROUPS - 1, GROUPS // 2 - 1, 1)

            with dve.Fori(0, NB) as n:
                chain.enter(2 * (4 * CHUNK + 1), n)
                for c in range(2):
                    dve.wait_ge(pair_in[c], 32 * (n + 1))
                    dve.wait_ge(final_ready[c], n)
                    for k, src in enumerate((resid[c], mixed[c])):
                        for t in range(CHUNK):
                            gate = gates[:, bass.ds(2 * n + c, 1), t, k]
                            then(dve.scalar_tensor_tensor(
                                out=mixed[c][:, t, :], in0=pair[c][:, t, k * D:(k + 1) * D], scalar=gate,
                                in1=src[:, t, :], op0=ALU.mult, op1=ALU.add))
                        sync()
                    for t in range(CHUNK):
                        then(dve.bn_stats(stats[:, c, t, :], mixed[c][:, t, :]))
                    sync()
                    hold()
                    for t in range(CHUNK):
                        then(dve.bn_aggr(mean_var[:, c, t, :], stats[:, c, t, :]))
                    sync()
                    then(dve.tensor_scalar(minus_mean[:, c, :], mean_var[:, c, :, 0], -1.0, None, ALU.mult))
                    dve.tensor_scalar(var[:, c, :], mean_var[:, c, :, 1], EPS, None, ALU.add).then_inc(fv_ready, 1)
            chain.leave(NB)


_INS = ["L0_attn_x", "L0_attn_w_q", "L0_attn_b_q", "L0_attn_w_k", "L0_attn_b_k", "L0_attn_w_v", "L0_attn_b_v",
        "L0_attn_w_out", "L0_attn_b_out", "L0_ffn_Wr", "L0_ffn_br", "L0_ffn_W1", "L0_ffn_b1", "L0_ffn_g1",
        "L0_ffn_be1", "L0_ffn_W2", "L0_ffn_b2"]


def kernel(**inputs):
    import numpy as _np
    import concourse.bacc as _bacc
    from concourse import mybir as _mybir
    from concourse.bass_utils import run_bass_kernel_spmd as _run

    nc = _bacc.Bacc("TRN2", target_bir_lowering=False, num_devices=1)
    arrays, args = {}, []
    for name in _INS:
        a = _np.ascontiguousarray(inputs[name])
        arrays[f"in_{name}_dram"] = a
        args.append(nc.dram_tensor(f"in_{name}_dram", a.shape, _mybir.dt.from_np(a.dtype), kind="ExternalInput").ap())
    shape = inputs["L0_attn_x"].shape
    out = nc.dram_tensor("out_0_dram", shape, _mybir.dt.float32, kind="ExternalOutput").ap()
    post_ln_moe_layer(nc, *args, out)
    r = _run(nc, [arrays], core_ids=[0])
    return r.results[0]["out_0_dram"]
```

```python
from contextlib import ExitStack

import concourse.bass as bass
from concourse import mybir

F32 = mybir.dt.float32
F32R = mybir.dt.float32r
BF16 = mybir.dt.bfloat16
I32 = mybir.dt.int32
U32 = mybir.dt.uint32
ALU = mybir.AluOpType
ACT = mybir.ActivationFunctionType
AX = mybir.AxisListType

P = 128
EPS = 1e-5


def wait(engine, sem, value):
    if isinstance(value, int) and value <= 0:
        return
    engine.wait_ge(sem, value)


class Chain:

    def __init__(self, engine, sem):
        self.engine, self.sem, self.base, self.steps = engine, sem, 0, 0

    def then(self, instruction):
        instruction.then_inc(self.sem, 1)
        self.steps += 1

    def sync(self, behind=0):
        wait(self.engine, self.sem, self.base + self.steps - behind)

    def enter(self, per_iteration, i):
        self.outer, self.per = self.base + self.steps, per_iteration
        self.base, self.steps = self.outer + i * per_iteration, 0

    def leave(self, iterations):
        assert self.steps == self.per, self.steps
        self.base, self.steps = self.outer + iterations * self.per, 0


class Group:

    def __init__(self, number, fours, quarter):
        self.number, self.fours, self.quarter = number, fours, quarter
        self.parity, self.pairs = quarter % 2, 2 * fours + quarter // 2

    def ahead(self, d):
        q = self.quarter + d
        return Group(self.number + d, self.fours + q // 4, q % 4)

    def within(self, groups):
        return not isinstance(self.number, int) or 0 <= self.number < groups


def walk_groups(engine, groups, step, lead, tail, enter=None, leave=None):
    for s in range(-lead, 4):
        step(Group(s, s // 4, s % 4))
    fours = groups // 4 - 2
    with engine.Fori(0, fours) as i:
        if enter:
            enter(i)
        for q in range(4):
            step(Group(4 * i + 4 + q, i + 1, q))
    if leave:
        leave(fours)
    for s in range(groups - 4, groups + tail):
        step(Group(s, s // 4, s % 4))


def post_ln_moe_layer(nc, x, w_q, b_q, w_k, b_k, w_v, b_v, w_out, b_out,
                      w_r, b_r, w_1, b_1, g_1, be_1, w_2, b_2, out):
    NB, S, D = x.shape
    E = w_r.shape[1]
    H = w_1.shape[2]
    N = NB * S
    TILES = S // P
    CHUNK = 4
    CHUNKS = NB * TILES // CHUNK
    CW = CHUNK * P
    KT = S // P
    assert D == P and H == P and TILES == 2 * CHUNK and NB % 2 == 0
    SCALE = float(D) ** -0.5
    REGION = N + P
    ROW = D + 4
    EXPERT_TILES = -(-(2 * N // P + E) // CHUNK) * CHUNK
    GROUPS = EXPERT_TILES // CHUNK
    assert GROUPS % 4 == 0 and GROUPS >= 12 and EXPERT_TILES <= 2 * P

    with ExitStack() as ctx, ExitStack() as late:
        def sb(name, shape, dt=F32, stack=None):
            return (stack or ctx).enter_context(nc.sbuf_tensor(name, shape, dt))

        def sem(name):
            return ctx.enter_context(nc.semaphore(name))

        routed = nc.dram_tensor("routed_rows", [E * REGION, ROW], F32).ap()
        chosen = nc.dram_tensor("expert_rows", [2 * N, D], F32).ap()

        x_v = x.rearrange("n (p j) d -> n p j d", p=P)
        out_v = out.rearrange("n (p c j) d -> n c p j d", p=P, c=2)
        chosen_v = chosen.rearrange("(n p c j k) d -> n c p j k d", n=NB, p=P, c=2, k=2)

        ident = sb("ident", [P, P])
        partition = sb("partition", [P, 1])
        column = sb("column", [P, P])
        expert_ids = sb("expert_ids", [P, E])
        w1_sb = sb("w1_sb", [P, E, H])
        w2_sb = sb("w2_sb", [P, E, D])
        b1_bc = sb("b1_bc", [P, E, H])
        b2_row = sb("b2_row", [1, E, D])
        ones = sb("ones", [P, P])
        x1_all = sb("x1_all", [P, CHUNKS, CHUNK, D])
        g_rows = sb("g_rows", [E, 2, H])
        g_cols = sb("g_cols", [P, 2, E])
        minus_half = sb("minus_half", [P, CHUNK])
        region_start = sb("region_start", [P, E])
        pad_row = sb("pad_row", [P, ROW])
        base = sb("base", [P, 2, E])
        base_i = sb("base_i", [P, E], I32)
        tile_table = sb("tile_table", [1, 4 * P], I32)
        var = sb("var", [P, 2, CHUNK])
        rstd = sb("rstd", [P, 2, CHUNK])
        stats = sb("stats", [P, 2, CHUNK, 6])
        mean_var = sb("mean_var", [P, 2, CHUNK, 2])
        tab = sb("tab", [P, 8, E])
        tab_i = sb("tab_i", [P, E], I32)
        per_tile = sb("per_tile", [P, 2, E])
        per_tile2 = sb("per_tile2", [P, 2, E])
        tile_cols = sb("tile_cols", [P, 4])
        expert_cols = sb("expert_cols", [P, 2, P])
        expert_of_tile = sb("expert_of_tile", [P, 2 * P])

        with ExitStack() as early:
            def sb1(name, shape, dt=F32):
                return sb(name, shape, dt, early)

            w_rows = [sb1(f"w_rows{i}", [P, D]) for i in range(4)]
            wT = sb1("wT", [P, 2, D])
            woutT = sb1("woutT", [P, D])
            wvo = sb1("wvo", [P, D])
            bq = sb1("bq", [P, 1])
            bk = sb1("bk", [P, 1])
            bv = sb1("bv", [P, 1])
            bv_cols = sb1("bv_cols", [P, P])
            bout_bc = sb1("bout_bc", [P, D])
            bvo_bc = sb1("bvo_bc", [P, D])
            wr_sb = sb1("wr_sb", [P, E])
            br_bc = sb1("br_bc", [P, E])
            iota_i = sb1("iota_i", [P, P + 1], I32)
            before = sb1("before", [P, P], BF16)
            ones_h = sb1("ones_h", [P, P], BF16)
            row_ids = sb1("row_ids", [P, 2, CHUNK])

            x_tok = [sb1(f"x_tok{i}", [P, TILES, D]) for i in range(2)]
            xT = sb1("xT", [P, S])
            qkT_hi = [[sb1(f"{n}T_hi{i}", [P, S], F32R) for n in "qk"] for i in range(2)]
            qkT_lo = [[sb1(f"{n}T_lo{i}", [P, S], F32R) for n in "qk"] for i in range(2)]
            v = [sb1(f"v{i}", [P, KT, D]) for i in range(2)]
            minus_max = sb1("minus_max", [P, 2])
            probs = [sb1(f"probs{i}", [P, S]) for i in range(2)]
            total = sb1("total", [P, 2 * TILES])
            inv_total = sb1("inv_total", [P, CHUNK])
            pT = [sb1(f"pT{i}", [P, KT, CW]) for i in range(2)]
            attnT = sb1("attnT", [P, CW])
            x_res = [sb1(f"x_res{i}", [P, CHUNK, D]) for i in range(2)]
            summed = sb1("summed", [P, CHUNK, D])
            x1 = [sb1(f"x1_{i}", [P, CHUNK, ROW]) for i in range(2)]
            x1T = sb1("x1T", [P, CW])
            logits = sb1("logits", [P, CHUNK, E])
            top = sb1("top", [P, CHUNK, 8])
            top_i = sb1("top_i", [P, CHUNK, 8], U32)
            top_f = sb1("top_f", [P, CHUNK, 2])
            picked = sb1("picked", [P, 2, CHUNK, E])
            picked_h = sb1("picked_h", [P, CHUNK + 1, E], BF16)
            shifted = sb1("shifted", [P, CHUNK, E + 2])
            expd = sb1("expd", [P, CHUNK, E + 2])
            gate_sum = sb1("gate_sum", [P, 4, CHUNK])
            gate_p = sb1("gate_p", [P, CHUNK, 2])
            rank = sb1("rank", [P, CHUNK, E])
            rank_k = sb1("rank_k", [P, 2, CHUNK, E])
            place_f = sb1("place_f", [P, 2, CHUNK])
            place = [sb1(f"place{i}", [P, 2, CHUNK], U32) for i in range(2)]

        def sb2(name, shape, dt=F32):
            return sb(name, shape, dt, late)

        row_in = [sb2(f"row_in{i}", [P, CHUNK, ROW]) for i in range(4)]
        inT = [sb2(f"inT{i}", [P, CW]) for i in range(2)]
        hidden = [sb2(f"hidden{i}", [P, CHUNK, H]) for i in range(2)]
        normed = [sb2(f"normed{i}", [P, CHUNK, H]) for i in range(2)]
        actT = [sb2(f"actT{i}", [P, CW]) for i in range(2)]
        row_out = [sb2(f"row_out{i}", [P, CHUNK, D]) for i in range(2)]
        is_second = sb2("is_second", [P, CHUNK])
        dest_f = sb2("dest_f", [P, CHUNK])
        gate_part = sb2("gate_part", [P, 3, CHUNK])
        dest = [sb2(f"dest{i}", [P, CHUNK], U32) for i in range(4)]
        gate = [sb2(f"gate{i}", [P, CHUNK]) for i in range(4)]
        pair = [sb2(f"pair{i}", [P, CHUNK, 2, D]) for i in range(2)]
        mixed = [sb2(f"mixed{i}", [P, CHUNK, D]) for i in range(2)]
        total_row = [sb2(f"total_row{i}", [P, CHUNK, D]) for i in range(2)]
        shift = sb2("shift", [P, 2, CHUNK])
        minus_mean = sb2("minus_mean", [P, 2, CHUNK])
        final = [sb2(f"final{i}", [P, CHUNK, D]) for i in range(2)]

        scores = [ctx.enter_context(nc.psum_tensor(f"scores{i}", [P, 2, 512], F32)) for i in range(2)]
        turned = ctx.enter_context(nc.psum_tensor("turned", [P, 2, 512], F32))
        value_sum = ctx.enter_context(nc.psum_tensor("value_sum", [P, 512], F32))
        work = ctx.enter_context(nc.psum_tensor("work", [P, 512], F32))

        (weights_in, consts_in, expert_in, iota_done, ident_ready, setup_pe, setup_dve,
         proj_filled, proj_split, proj_taken, scores_ready, max_ready, probs_ready, turned_ready,
         pT_ready, values_ready, attnT_copied, attn_ready, attn_taken,
         var_ready, rstd_ready, x1_ready, x1_turned, x1T_ready, logits_ready, logits_taken,
         mask_ready, exp_ready, rank_ready, rank_taken, place_ready, pad_ready, pad_in,
         table_pe, table_ready, pool_const, cols_ready) = [sem(n) for n in (
             "weights_in consts_in expert_in iota_done ident_ready setup_pe setup_dve "
             "proj_filled proj_split proj_taken scores_ready max_ready probs_ready turned_ready "
             "pT_ready values_ready attnT_copied attn_ready attn_taken "
             "var_ready rstd_ready x1_ready x1_turned x1T_ready logits_ready logits_taken "
             "mask_ready exp_ready rank_ready rank_taken place_ready pad_ready pad_in "
             "table_pe table_ready pool_const cols_ready").split()]
        x_in = [sem(f"x_in{i}") for i in range(2)]
        res_in = [sem(f"res_in{i}") for i in range(2)]
        scattered = [sem(f"scattered{i}") for i in range(2)]
        x1_kept = sem("x1_kept")
        rows_in = [sem(f"rows_in{i}") for i in range(4)]
        (in_turned, inT_ready, hidden_ready, ev_ready, er_ready, normed_ready, norm_turned,
         actT_ready, result_ready) = [sem(n) for n in (
             "in_turned inT_ready hidden_ready ev_ready er_ready normed_ready norm_turned "
             "actT_ready result_ready").split()]
        result_taken, gate_ready = sem("result_taken"), sem("gate_ready")
        delivered = [sem(f"delivered{i}") for i in range(2)]
        pair_in = [sem(f"pair_in{i}") for i in range(2)]
        pair_mixed, fv_ready, fr_ready, final_ready = [sem(n) for n in "pair_mixed fv_ready fr_ready final_ready".split()]
        final_out = [sem(f"final_out{i}") for i in range(2)]
        dve_chain, dve_held, pool_held = sem("dve_chain"), sem("dve_held"), sem("pool_held")

        BATCH_LOOPS = (NB - 4) // 2

        def live(chunk):
            return not isinstance(chunk, int) or chunk >= 0

        block = ctx.enter_context(nc.Block())

        def expert_registers(engine, name, groups):
            return [engine.alloc_register(f"{name}{i}") for i in range(CHUNK * groups)]

        def load_experts(engine, registers, group):
            n = len(registers)
            engine.load(registers, tile_table[0:1, bass.ds(group * CHUNK, n)])
            return [engine.snap(r, min_val=0, max_val=E - 1) for r in registers]

        @block.sync
        def _(sp):
            sp.dma_start(x_tok[0][:], x_v[0]).then_inc(x_in[0], 16)
            for i, w in enumerate((w_q, w_k, w_v, w_out)):
                sp.dma_start(w_rows[i][:], w).then_inc(weights_in, 16)
            for dst, b in ((bq, b_q), (bk, b_k), (bv, b_v)):
                sp.dma_start(dst[:], b.rearrange("(d a) -> d a", a=1)).then_inc(consts_in, 16)
            sp.dma_start(bout_bc[:], b_out.rearrange("(a d) -> a d", a=1).to_broadcast([P, D])).then_inc(consts_in, 16)
            sp.dma_start(wr_sb[:], w_r).then_inc(consts_in, 16)
            sp.dma_start(br_bc[:], b_r.rearrange("(a d) -> a d", a=1).to_broadcast([P, E])).then_inc(consts_in, 16)
            sp.dma_start(x_tok[1][:], x_v[1]).then_inc(x_in[1], 16)
            sp.dma_start(g_rows[:, 0, :], g_1).then_inc(expert_in, 16)
            sp.dma_start(g_rows[:, 1, :], be_1).then_inc(expert_in, 16)
            sp.dma_start(w1_sb[:], w_1.rearrange("e i h -> i e h")).then_inc(expert_in, 16)
            sp.dma_start(w2_sb[:], w_2.rearrange("e i h -> i e h")).then_inc(expert_in, 16)
            sp.dma_start(b1_bc[:], b_1.rearrange("(a e) h -> a e h", a=1).to_broadcast([P, E, H])).then_inc(expert_in, 16)
            sp.dma_start(b2_row[:], b_2.rearrange("(a e) h -> a e h", a=1)).then_inc(expert_in, 16)

            def batch(n, p, load=True):
                for c in range(2):
                    wait(sp, attn_taken, 2 * n + c - 1)
                    sp.dma_start(x_res[c][:], x_v[n][:, CHUNK * c:CHUNK * (c + 1), :]).then_inc(res_in[c], 16)
                if load:
                    wait(sp, proj_filled, 8 * n + 2)
                    sp.dma_start(x_tok[p][:], x_v[n + 2]).then_inc(x_in[p], 16)

            batch(0, 0)
            with sp.Fori(0, BATCH_LOOPS) as i:
                batch(2 * i + 1, 1)
                batch(2 * i + 2, 0)
            batch(NB - 3, 1)
            batch(NB - 2, 0, load=False)
            batch(NB - 1, 1, load=False)

            ends = [sp.alloc_register(f"end{i}") for i in range(4)]
            sp.wait_ge(pad_ready, 1)
            for e0 in range(0, E, 4):
                sp.load(ends, base_i[0:1, e0:e0 + 4])
                for i, r in enumerate(ends):
                    e = e0 + i
                    start = sp.snap(r, min_val=e * REGION, max_val=e * REGION + N)
                    sp.dma_start(routed[bass.ds(start, P), :], pad_row[:]).then_inc(pad_in, 16)
            sp.wait_ge(table_ready, 1)
            sp.wait_ge(pad_in, 16 * E)
            for c in range(2):
                sp.wait_ge(scattered[c], 16 * 2 * CHUNK * (CHUNKS // 2))

            row_registers = [sp.alloc_register(f"row{i}") for i in range(CHUNK)]

            def rows(g):
                if not g.within(GROUPS):
                    return
                sp.load(row_registers, tile_table[0:1, bass.ds(g.number * CHUNK + 2 * P, CHUNK)])
                wait(sp, in_turned, g.number - 3)
                wait(sp, ev_ready, g.number - 3)
                for t, r in enumerate(row_registers):
                    row = sp.snap(r, min_val=0, max_val=E * REGION - P)
                    sp.dma_start(row_in[g.quarter][:, t, :],
                                 routed[bass.ds(row, P), :]).then_inc(rows_in[g.quarter], 16)

            walk_groups(sp, GROUPS, rows, 0, 0)

            for p in range(2):
                sp.wait_ge(delivered[p], 16 * CHUNK * (GROUPS // 2))

            def pair_rows(n, c):
                wait(sp, pair_mixed, 2 * n + c - 1)
                sp.dma_start(pair[c][:], chosen_v[n][c]).then_inc(pair_in[c], 16)

            def store(n, c):
                sp.wait_ge(final_ready, 2 * n + c + 1)
                sp.dma_start(out_v[n][c], final[c][:]).then_inc(final_out[c], 16)

            pair_rows(0, 0)
            pair_rows(0, 1)
            pair_rows(1, 0)
            pair_rows(1, 1)
            with sp.Fori(0, NB - 2) as n:
                for c in range(2):
                    store(n, c)
                    pair_rows(n + 2, c)
            for n in range(NB - 2, NB):
                for c in range(2):
                    store(n, c)
            for c in range(2):
                sp.wait_ge(final_out[c], 16 * NB)

        @block.gpsimd
        def _(pool):
            def hold():
                pool.sem_inc(pool_held, 1)

            pool.iota(iota_i[:, 0:P], [[1, P]], base=0, channel_multiplier=0).then_inc(iota_done, 1)
            pool.iota(iota_i[:, P:P + 1], [[1, 1]], base=0, channel_multiplier=1).then_inc(iota_done, 1)
            pool.memset(minus_half[:], -0.5).then_inc(pool_const, 1)
            pool.memset(ones_h[:], 1.0).then_inc(pool_const, 1)
            pool.memset(pad_row[:], 0.0).then_inc(pool_const, 1)
            pool.memset(x1[0][:], 0.0).then_inc(pool_const, 1)
            pool.memset(x1[1][:], 0.0).then_inc(pool_const, 1)
            pool.wait_ge(pool_const, 5)

            def scale(C):
                pool.wait_ge(var_ready, C + 1)
                pool.tensor_tensor(rstd[:, 0, :], var[:, 0, :], minus_half[:], ALU.pow).then_inc(rstd_ready, 1)

            def scatter(C, c):
                pool.wait_ge(place_ready, C + 1)
                hold()
                for t in range(CHUNK):
                    for s in range(2):
                        pool.indirect_dma_start(
                            routed, bass.IndirectOffsetOnAxis(ap=place[c][:, s, t:t + 1], axis=0),
                            x1[c][:, t, :], None).then_inc(scattered[c], 16)

            scale(0)
            with pool.Fori(0, CHUNKS // 2 - 1) as i:
                for c in range(2):
                    scale(2 * i + c + 1)
                    scatter(2 * i + c, c)
            scale(CHUNKS - 1)
            scatter(CHUNKS - 2, 0)
            scatter(CHUNKS - 1, 1)

            def expert_step(g):
                if g.within(GROUPS):
                    pool.wait_ge(ev_ready, g.number + 1)
                    wait(pool, normed_ready, g.number - 1)
                    pool.tensor_tensor(rstd[:, g.parity, :], var[:, g.parity, :], minus_half[:],
                                       ALU.pow).then_inc(er_ready, 1)
                g = g.ahead(-2)
                if g.within(GROUPS):
                    pool.wait_ge(result_taken, g.number + 1)
                    hold()
                    for t in range(CHUNK):
                        pool.indirect_dma_start(
                            chosen, bass.IndirectOffsetOnAxis(ap=dest[g.quarter][:, t:t + 1], axis=0),
                            row_out[g.parity][:, t, :], None, bounds_check=2 * N - 1,
                            oob_is_err=False).then_inc(delivered[g.parity], 16)

            walk_groups(pool, GROUPS, expert_step, 0, 2)

            def mix(k, n, c):
                pool.wait_ge(pair_in[c], 16 * (n + 1))
                wait(pool, fv_ready, k - 1)
                pool.tensor_tensor(mixed[c][:], pair[c][:, :, 0, :], pair[c][:, :, 1, :],
                                   ALU.add).then_inc(pair_mixed, 1)

            def scale(k, c):
                pool.wait_ge(fv_ready, k + 1)
                wait(pool, final_ready, k - 1)
                pool.tensor_tensor(rstd[:, c, :], var[:, c, :], minus_half[:], ALU.pow).then_inc(fr_ready, 1)
                pool.wait_ge(fr_ready, 2 * k + 1)
                pool.tensor_tensor(shift[:, c, :], minus_mean[:, c, :], rstd[:, c, :],
                                   ALU.mult).then_inc(fr_ready, 1)

            def pair_of_chunks(n):
                mix(2 * n + 1, n, 1)
                scale(2 * n, 0)
                mix(2 * n + 2, n + 1, 0)
                scale(2 * n + 1, 1)

            mix(0, 0, 0)
            pair_of_chunks(0)
            with pool.Fori(0, NB - 2) as i:
                pair_of_chunks(i + 1)
            mix(2 * NB - 1, NB - 1, 1)
            scale(2 * NB - 2, 0)
            scale(2 * NB - 1, 1)

        @block.tensor
        def _(pe):
            pe.wait_ge(weights_in, 64)
            pe.wait_ge(ident_ready, 1)
            for i, src in enumerate((0, 1, 3)):
                mm = pe.transpose(work[:, i * P:(i + 1) * P], w_rows[src][:], ident[:])
            mm.then_inc(setup_pe, 1)
            pe.wait_ge(setup_dve, 1)
            pe.matmul(value_sum[:, 0:D], w_rows[2][:], woutT[:], start=True, stop=True)
            pe.matmul(value_sum[:, D:2 * D], bv_cols[:], woutT[:], start=True, stop=True)
            pe.wait_ge(expert_in, 96)
            for i in range(2):
                mm = pe.transpose(value_sum[:, 2 * D + i * E:2 * D + (i + 1) * E], g_rows[:, i, :], ident[0:E, 0:E])
            mm.then_inc(setup_pe, 1)
            pe.wait_ge(setup_dve, 4)

            def three_passes(dst, a_hi, a_lo, b_hi, b_lo, start=True, stop=True):
                pe.matmul(dst, a_hi, b_hi, start=start, stop=False)
                pe.matmul(dst, a_hi, b_lo, start=False, stop=False)
                return pe.matmul(dst, a_lo, b_hi, start=False, stop=stop)

            def project(n, m, p, j):
                h = j % 2
                cols = slice(h * CW, (h + 1) * CW)
                if j < 2:
                    pe.wait_ge(x_in[p], 16 * (m + 1))
                    for t in range(CHUNK):
                        mm = pe.transpose(work[:, t * P:(t + 1) * P], x_tok[p][:, h * CHUNK + t, :], ident[:])
                elif j < 6:
                    k = (j - 2) // 2
                    pe.wait_ge(proj_taken, 8 * n + 2)
                    mm = pe.matmul(work[:], wT[:, k, :], xT[:, cols], start=True, stop=True)
                else:
                    for t in range(CHUNK):
                        mm = pe.matmul(work[:, t * D:(t + 1) * D],
                                       xT[:, h * CW + t * P:h * CW + (t + 1) * P], wvo[:], start=True, stop=True)
                mm.then_inc(proj_filled, 1)

            def score(s, p, j):
                wait(pe, probs_ready, s - 1)
                q = slice(j * P, (j + 1) * P)
                for h in range(2):
                    k = slice(h * CW, (h + 1) * CW)
                    mm = three_passes(scores[j % 2][:, h, :], qkT_hi[p][0][:, q], qkT_lo[p][0][:, q],
                                      qkT_hi[p][1][:, k], qkT_lo[p][1][:, k])
                mm.then_inc(scores_ready, 1)

            def turn(s, j):
                pe.wait_ge(probs_ready, s + 1)
                for h in range(2):
                    wait(pe, pT_ready, 2 * (s - 1) + h + 1)
                    for t in range(4):
                        k = 4 * h + t
                        mm = pe.transpose(turned[:, h, t * P:(t + 1) * P],
                                          probs[j % 2][:, k * P:(k + 1) * P], ident[:])
                    mm.then_inc(turned_ready, 1)

            def weigh(C, c, vp, r):
                if r == 0:
                    pe.wait_ge(pT_ready, 8 * (C + 1))
                    wait(pe, attnT_copied, C)
                for k in (2 * r, 2 * r + 1):
                    mm = pe.matmul(value_sum[:], v[vp][:, k, :], pT[c][:, k, :], start=(k == 0), stop=(k == KT - 1))
                if r == 3:
                    mm.then_inc(values_ready, 1)

            def turn_back(C):
                pe.wait_ge(attnT_copied, C + 1)
                for t in range(CHUNK):
                    mm = pe.transpose(work[:, t * P:(t + 1) * P], attnT[:, t * P:(t + 1) * P], ident[:])
                mm.then_inc(attn_ready, 1)

            def turn_x1(C, c):
                pe.wait_ge(x1_ready, C + 1)
                for t in range(CHUNK):
                    mm = pe.transpose(work[:, t * P:(t + 1) * P], x1[c][:, t, 0:D], ident[:])
                mm.then_inc(x1_turned, 1)

            def router(C):
                pe.wait_ge(x1T_ready, C + 1)
                for t in range(CHUNK):
                    mm = pe.matmul(work[:, t * E:(t + 1) * E], x1T[:, t * P:(t + 1) * P], wr_sb[:],
                                   start=True, stop=True)
                mm.then_inc(logits_ready, 1)

            def rank_picks(C):
                pe.wait_ge(mask_ready, C + 1)
                pe.matmul(work[:, 0:(CHUNK + 1) * E], before[:], picked_h[:].rearrange("p t e -> p (t e)"),
                          start=True, stop=False)
                for t in range(CHUNK):
                    after = CHUNK - t
                    mm = pe.matmul(work[:, (t + 1) * E:(CHUNK + 1) * E].rearrange("p (t e) -> p t e", t=after),
                                   ones_h[:], picked_h[:, t:t + 1, :].to_broadcast([P, after, E]),
                                   start=False, stop=(t == CHUNK - 1))
                mm.then_inc(rank_ready, 1)

            def route(C, c, r):
                if r == 0 and live(C - 2):
                    turn_back(C - 2)
                if r == 1 and live(C - 3):
                    rank_picks(C - 3)
                if r == 2 and live(C - 2):
                    turn_x1(C - 2, c)
                if r == 3 and live(C - 2):
                    router(C - 2)

            def work_free(C, r):
                if r == 0:
                    wait(pe, logits_taken, C - 2)
                if r == 1:
                    wait(pe, attn_taken, C - 1)
                if r == 2:
                    wait(pe, rank_taken, C - 2)
                if r == 3:
                    wait(pe, x1T_ready, C - 1)

            def batch(n, m, p, score_next=True, project_next=True):
                for j in range(TILES):
                    c, r = j // CHUNK, j % CHUNK
                    s, C = TILES * n + j, 2 * n + c
                    turn(s, j)
                    if j < TILES - 1:
                        score(s + 1, p, j + 1)
                    elif score_next:
                        pe.wait_ge(proj_taken, 8 * (n + 1) + 6)
                        score(s + 1, 1 - p, 0)
                    if project_next:
                        if isinstance(n, int):
                            pe.wait_ge(proj_taken, 8 * (n + 1) + j)
                        work_free(C, r)
                        project(n + 1, m + p, 1 - p, j)
                    if live(C - 1):
                        if r == 0 and c == 1:
                            pe.wait_ge(proj_taken, 8 * (n + 1))
                        weigh(C - 1, 1 - c, (1 - p) if c == 0 else p, r)
                    if project_next:
                        if live(C - 2):
                            pe.wait_ge(proj_taken, 8 * (n + 1) + j + 1)
                    else:
                        work_free(C, r)
                    route(C, c, r)

            for j in range(TILES):
                if j:
                    pe.wait_ge(proj_taken, j)
                project(0, 0, 0, j)
            pe.wait_ge(proj_taken, 8)
            score(0, 0, 0)
            batch(0, 0, 0)
            batch(1, 0, 1)
            with pe.Fori(0, BATCH_LOOPS) as i:
                batch(2 * i + 2, i + 1, 0)
                batch(2 * i + 3, i + 1, 1)
            batch(NB - 2, NB // 2 - 1, 0)
            batch(NB - 1, NB // 2 - 1, 1, score_next=False, project_next=False)
            for C in (CHUNKS, CHUNKS + 1):
                for r in range(4):
                    if C == CHUNKS:
                        weigh(C - 1, 1, 1, r)
                    work_free(C, r)
                    route(C, C % 2, r)
            work_free(CHUNKS + 2, 0)
            rank_picks(CHUNKS - 1)

            pe.wait_ge(cols_ready, 2)
            for i in range(4):
                mm = pe.matmul(work[0:1, i * P:(i + 1) * P], tile_cols[:, i:i + 1], ident[:], start=True, stop=True)
            mm.then_inc(table_pe, 1)
            pe.wait_ge(cols_ready, 4)
            for i in range(2):
                mm = pe.matmul(value_sum[:, i * P:(i + 1) * P], expert_cols[:, i, :], ident[:], start=True, stop=True)
            mm.then_inc(table_pe, 1)
            pe.wait_ge(table_ready, 1)
            registers = expert_registers(pe, "expert", 3)

            def turn_rows(g):
                pe.wait_ge(rows_in[g.quarter], 16 * CHUNK * (g.fours + 1))
                wait(pe, inT_ready, g.number - 1)
                for t in range(CHUNK):
                    mm = pe.transpose(scores[g.parity][:, 0, t * P:(t + 1) * P], row_in[g.quarter][:, t, 0:D], ident[:])
                mm.then_inc(in_turned, 1)

            def first_product(g, experts):
                p = g.parity
                pe.wait_ge(inT_ready, g.number + 1)
                wait(pe, ev_ready, g.number - 1)
                for t in range(CHUNK):
                    mm = pe.matmul(scores[p][:, 1, t * H:(t + 1) * H], inT[p][:, t * P:(t + 1) * P],
                                   w1_sb[:, bass.ds(experts[t], 1), :], start=True, stop=True)
                mm.then_inc(hidden_ready, 1)

            def turn_hidden(g):
                p = g.parity
                pe.wait_ge(normed_ready, g.number + 1)
                for t in range(CHUNK):
                    mm = pe.transpose(turned[:, p, t * P:(t + 1) * P], normed[p][:, t, :], ident[:])
                mm.then_inc(norm_turned, 1)

            def second_bias(g, experts):
                wait(pe, result_taken, g.number - 1)
                dst = (value_sum, work)[g.parity]
                for t in range(CHUNK):
                    pe.matmul(dst[:, t * D:(t + 1) * D], ones[0:1, :], b2_row[0:1, bass.ds(experts[t], 1), :],
                              start=(t == 0), stop=False)

            def second_product(g, experts):
                pe.wait_ge(actT_ready, g.number + 1)
                dst = (value_sum, work)[g.parity]
                for t in range(CHUNK):
                    mm = pe.matmul(dst[:, t * D:(t + 1) * D], actT[g.parity][:, t * P:(t + 1) * P],
                                   w2_sb[:, bass.ds(experts[t], 1), :], start=False, stop=(t == CHUNK - 1))
                mm.then_inc(result_ready, 1)

            def expert_step(g):
                last, after = g.ahead(-1), g.ahead(1)
                if isinstance(g.number, int):
                    start = min(max(last.number, 0), GROUPS - 3)
                    skip = last.number - start
                else:
                    start, skip = last.number, 0
                experts = load_experts(pe, registers, start)
                if last.within(GROUPS):
                    experts_last = experts[CHUNK * skip:]
                if after.within(GROUPS):
                    experts_after = experts[CHUNK * (skip + 2):]
                if last.within(GROUPS):
                    turn_hidden(last)
                    second_bias(last, experts_last)
                if after.within(GROUPS):
                    first_product(after, experts_after)
                if g.ahead(2).within(GROUPS):
                    turn_rows(g.ahead(2))
                if last.within(GROUPS):
                    second_product(last, experts_last)

            walk_groups(pe, GROUPS, expert_step, 2, 1)

        @block.scalar
        def _(act):
            act.preload_act_table(ACT.Exp)
            act.wait_ge(setup_dve, 4)

            def project(n, p, j):
                h = j % 2
                cols = slice(h * CW, (h + 1) * CW)
                if j < 6:
                    act.wait_ge(proj_filled, 8 * n + j + 1)
                if j < 2:
                    act.copy(xT[:, cols], work[:]).then_inc(proj_taken, 1)
                elif j < 6:
                    k = (j - 2) // 2
                    act.activation(qkT_hi[p][k][:, cols], work[:], ACT.Identity,
                                   bias=(bq, bk)[k][:, 0:1]).then_inc(proj_split, 1)

            def exponent(s, j, zp):
                act.wait_ge(max_ready, s + 1)
                wait(act, turned_ready, 2 * (s - 1))
                act.activation(probs[j % 2][:], scores[j % 2][:].rearrange("p a b -> p (a b)"), ACT.Exp,
                               bias=minus_max[:, j % 2:j % 2 + 1],
                               accum_out=total[:, zp * TILES + j:zp * TILES + j + 1]).then_inc(probs_ready, 1)

            def take_turned(s, C, c, r):
                if r == 0:
                    wait(act, values_ready, C - 1)
                for h in range(2):
                    act.wait_ge(turned_ready, 2 * s + h + 1)
                    act.copy(pT[c][:, 4 * h:4 * h + 4, r * P:(r + 1) * P],
                             turned[:, h, :].rearrange("p (k q) -> p k q", k=4)).then_inc(pT_ready, 1)

            def copy_values(C):
                act.wait_ge(values_ready, C + 1)
                wait(act, attn_ready, C)
                act.copy(attnT[:], value_sum[:]).then_inc(attnT_copied, 1)

            def route(C, c, r):
                if r == 1 and live(C - 3):
                    act.wait_ge(mask_ready, C - 2)
                    act.activation(expd[:], shifted[:], ACT.Exp).then_inc(exp_ready, 1)
                if r == 2 and live(C - 2):
                    act.wait_ge(x1_turned, C - 1)
                    wait(act, logits_ready, C - 2)
                    act.copy(x1T[:], work[:]).then_inc(x1T_ready, 1)
                    act.copy(x1_all[:, bass.ds(C - 2, 1), :, :].rearrange("p a t d -> p (a t) d"),
                             x1[c][:, :, 0:D]).then_inc(x1_kept, 1)
                if r == 3 and live(C - 1) and (not isinstance(C, int) or C <= CHUNKS):
                    copy_values(C - 1)

            def batch(n, p, score_next=True, project_next=True):
                for j in range(TILES):
                    c, r = j // CHUNK, j % CHUNK
                    s, C = TILES * n + j, 2 * n + c
                    take_turned(s, C, c, r)
                    if project_next:
                        project(n + 1, 1 - p, j)
                    if j < TILES - 1:
                        exponent(s + 1, j + 1, p)
                    elif score_next:
                        exponent(s + 1, 0, 1 - p)
                    route(C, c, r)

            for j in range(TILES):
                project(0, 0, j)
            exponent(0, 0, 0)
            batch(0, 0)
            batch(1, 1)
            with act.Fori(0, BATCH_LOOPS) as i:
                batch(2 * i + 2, 0)
                batch(2 * i + 3, 1)
            batch(NB - 2, 0)
            batch(NB - 1, 1, score_next=False, project_next=False)
            for C in (CHUNKS, CHUNKS + 1):
                for r in range(4):
                    route(C, C % 2, r)
            route(CHUNKS + 2, 0, 1)

            act.preload_act_table(ACT.Gelu)
            act.wait_ge(table_ready, 1)
            registers = expert_registers(act, "expert", 1)

            def take_rows(g):
                act.wait_ge(in_turned, g.number + 1)
                wait(act, hidden_ready, g.number - 1)
                act.copy(inT[g.parity][:], scores[g.parity][:, 0, :]).then_inc(inT_ready, 1)

            def gelu(g, experts):
                p = g.parity
                act.wait_ge(norm_turned, g.number + 1)
                for t in range(CHUNK):
                    a = act.activation(actT[p][:, t * P:(t + 1) * P], turned[:, p, t * P:(t + 1) * P], ACT.Gelu,
                                       bias=g_cols[:, 1, bass.ds(experts[t], 1)],
                                       scale=g_cols[:, 0, bass.ds(experts[t], 1)])
                a.then_inc(actT_ready, 1)

            def weigh_results(g):
                p = g.parity
                act.wait_ge(result_ready, g.number + 1)
                act.wait_ge(gate_ready, g.number + 1)
                if not isinstance(g.number, int) or g.number >= 2:
                    act.wait_ge(delivered[p], 16 * CHUNK * g.pairs)
                src = (value_sum, work)[p]
                for t in range(CHUNK):
                    a = act.activation(row_out[p][:, t, :], src[:, t * D:(t + 1) * D], ACT.Copy,
                                       scale=gate[g.quarter][:, t:t + 1])
                a.then_inc(result_taken, 1)

            def expert_step(g):
                if g.ahead(-2).within(GROUPS):
                    weigh_results(g.ahead(-2))
                last = g.ahead(-1)
                if last.within(GROUPS):
                    gelu(last, load_experts(act, registers, last.number))
                if g.ahead(2).within(GROUPS):
                    take_rows(g.ahead(2))

            walk_groups(act, GROUPS, expert_step, 2, 2)

            def normalise(k, n, c):
                act.wait_ge(fr_ready, 2 * k + 2)
                wait(act, final_out[c], 16 * n)
                for t in range(CHUNK):
                    a = act.activation(final[c][:, t, :], total_row[c][:, t, :], ACT.Identity,
                                       bias=shift[:, c, t:t + 1], scale=rstd[:, c, t:t + 1])
                a.then_inc(final_ready, 1)

            for c in range(2):
                normalise(c, 0, c)
            with act.Fori(0, NB - 1) as i:
                for c in range(2):
                    normalise(2 * i + 2 + c, i + 1, c)

        @block.vector
        def _(dve):
            chain = Chain(dve, dve_chain)
            then, sync = chain.then, chain.sync

            def hold():
                dve.sem_inc(dve_held, 1)


            dve.wait_ge(iota_done, 2)
            then(dve.tensor_copy(column[:], iota_i[:, 0:P]))
            then(dve.tensor_copy(partition[:], iota_i[:, P:P + 1]))
            then(dve.tensor_copy(expert_ids[:], iota_i[:, 0:E]))
            sync()
            dve.tensor_scalar(ident[:], column[:], partition[:, 0:1], None, ALU.is_equal).then_inc(ident_ready, 1)
            then(dve.tensor_scalar(before[:], column[:], partition[:, 0:1], None, ALU.is_gt))
            then(dve.memset(ones[:], 1.0))
            then(dve.memset(picked_h[:], 0.0))
            then(dve.tensor_scalar(region_start[:], expert_ids[:], float(REGION), None, ALU.mult))
            sync()
            then(dve.tensor_copy(base[:, 0, :], region_start[:]))
            for c in range(2):
                for t in range(CHUNK):
                    then(dve.tensor_scalar(row_ids[:, c, t:t + 1], partition[:], 2.0 * TILES,
                                           2.0 * (CHUNK * c + t), ALU.mult, ALU.add))
            dve.wait_ge(pool_const, 5)
            then(dve.memset(pad_row[:, D:D + 1], 2.0 * N))
            then(dve.memset(pad_row[:, D + 1:D + 2], -1.0))
            dve.wait_ge(consts_in, 96)
            then(dve.tensor_scalar(bq[:], bq[:], SCALE, None, ALU.mult))
            then(dve.tensor_scalar(bv_cols[:], ones[:], bv[:, 0:1], None, ALU.mult))
            dve.wait_ge(setup_pe, 1)
            then(dve.tensor_scalar(wT[:, 0, :], work[:, 0:D], SCALE, None, ALU.mult))
            then(dve.tensor_copy(wT[:, 1, :], work[:, D:2 * D]))
            dve.tensor_copy(woutT[:], work[:, 2 * D:3 * D]).then_inc(setup_dve, 1)
            dve.wait_ge(setup_pe, 2)
            dve.tensor_copy(wvo[:], value_sum[:, 0:D]).then_inc(setup_dve, 1)
            dve.tensor_tensor(bvo_bc[:], value_sum[:, D:2 * D], bout_bc[:], ALU.add).then_inc(setup_dve, 1)
            dve.tensor_copy(g_cols[:], value_sum[:, 2 * D:2 * D + 2 * E].rearrange("p (a e) -> p a e", a=2))\
                .then_inc(setup_dve, 1)
            dve.wait_ge(setup_dve, 4)
            sync()

            def project(n, p, j):
                h = j % 2
                cols = slice(h * CW, (h + 1) * CW)
                if 2 <= j < 6:
                    k = (j - 2) // 2
                    dve.wait_ge(proj_split, 4 * n + j - 1)
                    dve.scalar_tensor_tensor(out=qkT_lo[p][k][:, cols], in0=work[:], scalar=(bq, bk)[k][:, 0:1],
                                             in1=qkT_hi[p][k][:, cols].bitcast(F32), op0=ALU.add,
                                             op1=ALU.subtract).then_inc(proj_taken, 1)
                elif j >= 6:
                    dve.wait_ge(proj_filled, 8 * n + j + 1)
                    wait(dve, values_ready, 2 * (n - 2) + 2)
                    dve.tensor_tensor(v[p][:, h * CHUNK:(h + 1) * CHUNK, :],
                                      work[:].rearrange("p (t d) -> p t d", t=CHUNK),
                                      bvo_bc[:].rearrange("p (a d) -> p a d", a=1).to_broadcast([P, CHUNK, D]),
                                      ALU.add).then_inc(proj_taken, 1)

            def maximum(s, j):
                dve.wait_ge(scores_ready, s + 1)
                dve.tensor_reduce(minus_max[:, j % 2:j % 2 + 1], scores[j % 2][:], AX.XY, ALU.max,
                                  negate=True).then_inc(max_ready, 1)

            def attention_rows(C, c, zp, k):
                z = zp * TILES + c * CHUNK
                then(dve.reciprocal(inv_total[:], total[:, z:z + CHUNK]))
                sync()
                dve.wait_ge(attn_ready, C + 1)
                dve.wait_ge(res_in[c], 16 * (k + 1))
                for t in range(CHUNK):
                    a = dve.scalar_tensor_tensor(out=summed[:, t, :], in0=work[:, t * P:(t + 1) * P],
                                                 scalar=inv_total[:, t:t + 1], in1=x_res[c][:, t, :],
                                                 op0=ALU.mult, op1=ALU.add)
                    if t == CHUNK - 1:
                        a.then_inc(attn_taken, 1)
                dve.wait_ge(attn_taken, C + 1)
                for t in range(CHUNK):
                    then(dve.bn_stats(stats[:, 0, t, :], summed[:, t, :]))
                sync()
                hold()
                for t in range(CHUNK):
                    then(dve.bn_aggr(mean_var[:, 0, t, :], stats[:, 0, t, :]))
                sync()
                dve.tensor_scalar(var[:, 0, :], mean_var[:, 0, :, 1], EPS, None, ALU.add)\
                    .then_inc(var_ready, 1)
            def pick_experts(C, c):
                dve.wait_ge(logits_ready, C + 1)
                dve.tensor_tensor(logits[:], work[:, 0:CHUNK * E].rearrange("p (t e) -> p t e", t=CHUNK),
                                  br_bc[:].rearrange("p (a e) -> p a e", a=1).to_broadcast([P, CHUNK, E]),
                                  ALU.add).then_inc(logits_taken, 1)
                dve.wait_ge(logits_taken, C + 1)
                hold()
                for t in range(CHUNK):
                    then(dve.max(top[:, t, :], logits[:, t, :]))
                sync()
                hold()
                for t in range(CHUNK):
                    then(dve.max_index(top_i[:, t, :], top[:, t, :], logits[:, t, :]))
                largest = top[:, :, 0:1]
                then(dve.tensor_tensor(shifted[:, :, 0:E], logits[:], largest.to_broadcast([P, CHUNK, E]),
                                       ALU.subtract))
                then(dve.tensor_tensor(shifted[:, :, E:E + 2], top[:, :, 0:2],
                                       largest.to_broadcast([P, CHUNK, 2]), ALU.subtract))
                sync()
                then(dve.tensor_copy(top_f[:], top_i[:, :, 0:2]))
                sync()
                ids = expert_ids[:].rearrange("p (a e) -> p a e", a=1).to_broadcast([P, CHUNK, E])
                for s in range(2):
                    then(dve.tensor_tensor(picked[:, s], ids, top_f[:, :, s:s + 1].to_broadcast([P, CHUNK, E]),
                                           ALU.is_equal))
                sync()
                dve.tensor_tensor(picked_h[:, 0:CHUNK, :], picked[:, 0], picked[:, 1], ALU.add).then_inc(mask_ready, 1)
            def take_ranks(C, c):
                dve.wait_ge(rank_ready, C + 1)
                then(dve.tensor_tensor(base[:, 1 - c, :], base[:, c, :], work[:, CHUNK * E:(CHUNK + 1) * E], ALU.add))
                dve.tensor_tensor(rank[:], work[:, 0:CHUNK * E].rearrange("p (t e) -> p t e", t=CHUNK),
                                  base[:, c:c + 1, :].to_broadcast([P, CHUNK, E]), ALU.add).then_inc(rank_taken, 1)

            def place_rows(C, c):
                dve.wait_ge(exp_ready, C + 1)
                then(dve.tensor_reduce(gate_sum[:, 0, :], expd[:, :, 0:E], AX.X, ALU.add))
                dve.wait_ge(rank_taken, C + 1)
                for s in range(2):
                    then(dve.tensor_tensor(rank_k[:, s], picked[:, s], rank[:], ALU.mult))
                sync(behind=2)
                then(dve.reciprocal(gate_sum[:, 1, :], gate_sum[:, 0, :]))
                then(dve.tensor_copy(x1[c][:, :, D:D + 1], row_ids[:, c, :].rearrange("p (t a) -> p t a", a=1)))
                then(dve.tensor_copy(x1[c][:, :, D + 1:D + 2], top_f[:, :, 1:2]))
                sync(behind=2)
                then(dve.tensor_tensor(gate_p[:], expd[:, :, E:E + 2],
                                       gate_sum[:, 1, :].rearrange("p (t a) -> p t a", a=1).to_broadcast([P, CHUNK, 2]),
                                       ALU.mult))
                then(dve.tensor_reduce(place_f[:], rank_k[:], AX.X, ALU.add))
                sync(behind=1)
                then(dve.tensor_reduce(gate_sum[:, 2, :], gate_p[:], AX.X, ALU.add))
                sync(behind=1)
                then(dve.tensor_copy(place[c][:], place_f[:]))
                sync(behind=1)
                then(dve.tensor_scalar(gate_sum[:, 2, :], gate_sum[:, 2, :], 1e-9, None, ALU.max))
                then(dve.tensor_scalar(row_ids[:, c, :], row_ids[:, c, :], 2.0 * S, None, ALU.add))
                sync(behind=1)
                then(dve.reciprocal(gate_sum[:, 3, :], gate_sum[:, 2, :]))
                sync()
                dve.tensor_tensor(x1[c][:, :, D + 2:D + 4], gate_p[:],
                                  gate_sum[:, 3, :].rearrange("p (t a) -> p t a", a=1).to_broadcast([P, CHUNK, 2]),
                                  ALU.mult).then_inc(place_ready, 1)

            def normalise(C, c, k):
                dve.wait_ge(rstd_ready, C + 1)
                wait(dve, scattered[c], 16 * 2 * CHUNK * k)
                for t in range(CHUNK):
                    a = dve.tensor_scalar(x1[c][:, t, 0:D], summed[:, t, :], mean_var[:, 0, t, 0:1],
                                          rstd[:, 0, t:t + 1], ALU.subtract, ALU.mult)
                a.then_inc(x1_ready, 1)

            def route_before(C, c, r, zp, k):
                if r == 0 and live(C - 3):
                    pick_experts(C - 3, 1 - c)
                if r == 1 and live(C - 2):
                    attention_rows(C - 2, c, zp, k)
                if r == 2 and live(C - 3):
                    take_ranks(C - 3, 1 - c)

            def route_after(C, c, r, k):
                if r == 1 and live(C - 2):
                    normalise(C - 2, c, k)
                if r == 2 and live(C - 3):
                    place_rows(C - 3, 1 - c)

            def batch(n, p, score_next=True, project_next=True):
                for j in range(TILES):
                    c, r = j // CHUNK, j % CHUNK
                    s, C = TILES * n + j, 2 * n + c
                    route_before(C, c, r, 1 - p, n - 1)
                    if j < TILES - 1:
                        maximum(s + 1, j + 1)
                    elif score_next:
                        maximum(s + 1, 0)
                    if project_next:
                        project(n + 1, 1 - p, j)
                    route_after(C, c, r, n - 1)

            for j in range(TILES):
                project(0, 0, j)
            maximum(0, 0)
            batch(0, 0)
            batch(1, 1)
            with dve.Fori(0, BATCH_LOOPS) as i:
                chain.enter(4 * 36, i)
                batch(2 * i + 2, 0)
                batch(2 * i + 3, 1)
            chain.leave(BATCH_LOOPS)
            batch(NB - 2, 0)
            batch(NB - 1, 1, score_next=False, project_next=False)
            for C in (CHUNKS, CHUNKS + 1):
                for r in range(4):
                    route_before(C, C % 2, r, 1, NB - 1)
                    route_after(C, C % 2, r, NB - 1)
            pick_experts(CHUNKS - 1, 1)
            take_ranks(CHUNKS - 1, 1)
            place_rows(CHUNKS - 1, 1)

            sync()
            end = base[:, 0, :]
            dve.tensor_copy(base_i[:], end).then_inc(pad_ready, 1)
            count, count_i = tab[:, 0, :], tab_i
            then(dve.tensor_tensor(count, end, region_start[:], ALU.subtract))
            sync()
            then(dve.tensor_scalar(count, count, float(P - 1), None, ALU.add))
            sync()
            then(dve.tensor_copy(count_i[:], count))
            sync()
            then(dve.tensor_scalar(count_i[:], count_i[:], 7, None, ALU.logical_shift_right))
            sync()
            tiles = tab[:, 1, :]
            then(dve.tensor_copy(tiles, count_i[:]))
            upto = [tab[:, 2, :], tab[:, 3, :]]
            then(dve.tensor_copy(upto[0], count_i[:]))
            w = 1
            while w < E:
                sync()
                then(dve.tensor_tensor(upto[1][:, w:E], upto[0][:, w:E], upto[0][:, 0:E - w], ALU.add))
                then(dve.tensor_copy(upto[1][:, 0:w], upto[0][:, 0:w]))
                upto.reverse()
                w *= 2
            sync()
            for i in range(2):
                then(dve.tensor_scalar(tab[:, 4 + i, 0:1], partition[:], float(i * P), None, ALU.add))
            sync()
            for i in range(2):
                then(dve.tensor_scalar(per_tile[:, i, :], upto[0], tab[:, 4 + i, 0:1], None, ALU.is_le))
            sync()
            then(dve.tensor_tensor(per_tile2[:], per_tile[:],
                                   tiles.rearrange("p (a e) -> p a e", a=1).to_broadcast([P, 2, E]), ALU.mult))
            then(dve.tensor_reduce(tile_cols[:, 0:2], per_tile[:], AX.X, ALU.add))
            sync()
            then(dve.tensor_reduce(tab[:, 6, 0:2], per_tile2[:], AX.X, ALU.add))
            sync()
            for i in range(2):
                then(dve.tensor_tensor(tab[:, 7, i:i + 1], tab[:, 4 + i, 0:1], tab[:, 6, i:i + 1], ALU.subtract))
            sync()
            then(dve.tensor_scalar(tab[:, 7, 0:2], tab[:, 7, 0:2], float(P), None, ALU.mult))
            sync()
            then(dve.scalar_tensor_tensor(out=tab[:, 6, 0:2], in0=tile_cols[:, 0:2], scalar=float(REGION),
                                          in1=tab[:, 7, 0:2], op0=ALU.mult, op1=ALU.add))
            sync()
            dve.tensor_scalar(tile_cols[:, 2:4], tab[:, 6, 0:2], base[:, 0, E - 1:E], None,
                              ALU.min).then_inc(cols_ready, 1)
            dve.tensor_scalar(tile_cols[:, 0:2], tile_cols[:, 0:2], float(E - 1), None,
                              ALU.min).then_inc(cols_ready, 1)
            dve.wait_ge(cols_ready, 2)
            for i in range(2):
                dve.tensor_scalar(expert_cols[:, i, :], ones[:], tile_cols[:, i:i + 1], None,
                                  ALU.mult).then_inc(cols_ready, 1)
            dve.wait_ge(table_pe, 1)
            dve.tensor_copy(tile_table[:], work[0:1, :]).then_inc(table_ready, 1)
            dve.wait_ge(table_pe, 2)
            then(dve.tensor_copy(expert_of_tile[:], value_sum[:, 0:2 * P]))
            dve.wait_ge(table_ready, 1)
            sync()
            registers = expert_registers(dve, "expert", 1)

            def hidden_rows(g, experts):
                p, q = g.parity, g.quarter
                dve.wait_ge(hidden_ready, g.number + 1)
                wait(dve, normed_ready, g.number - 1)
                for t in range(CHUNK):
                    then(dve.tensor_tensor(hidden[p][:, t, :], scores[p][:, 1, t * H:(t + 1) * H],
                                           b1_bc[:, bass.ds(experts[t], 1), :].rearrange("p a h -> p (a h)"), ALU.add))
                column_of = lambda i: row_in[q][:, :, D + i]
                then(dve.tensor_tensor(is_second[:], column_of(1),
                                       expert_of_tile[:, bass.ds(g.number * CHUNK, CHUNK)], ALU.is_equal))
                sync(behind=1)
                for t in range(CHUNK):
                    then(dve.bn_stats(stats[:, p, t, :], hidden[p][:, t, :]))
                sync(behind=CHUNK)
                then(dve.tensor_tensor(dest_f[:], is_second[:], column_of(0), ALU.add))
                then(dve.tensor_tensor(gate_part[:, 0, :], is_second[:], column_of(3), ALU.mult))
                then(dve.tensor_tensor(gate_part[:, 1, :], is_second[:], column_of(2), ALU.mult))
                sync(behind=3)
                hold()
                for t in range(CHUNK):
                    then(dve.bn_aggr(mean_var[:, p, t, :], stats[:, p, t, :]))
                sync(behind=CHUNK)
                if not isinstance(g.number, int) or g.number >= 4:
                    dve.wait_ge(delivered[p], 16 * CHUNK * (g.pairs - 1))
                then(dve.tensor_copy(dest[q][:], dest_f[:]))
                then(dve.tensor_tensor(gate_part[:, 2, :], column_of(2), gate_part[:, 1, :], ALU.subtract))
                sync(behind=2)
                dve.tensor_scalar(var[:, p, :], mean_var[:, p, :, 1], EPS, None, ALU.add).then_inc(ev_ready, 1)
                sync()
                dve.tensor_tensor(gate[q][:], gate_part[:, 0, :], gate_part[:, 2, :], ALU.add).then_inc(gate_ready, 1)

            def norm_rows(g):
                p = g.parity
                dve.wait_ge(er_ready, g.number + 1)
                wait(dve, norm_turned, g.number - 1)
                for t in range(CHUNK):
                    a = dve.tensor_scalar(normed[p][:, t, :], hidden[p][:, t, :], mean_var[:, p, t, 0:1],
                                          rstd[:, p, t:t + 1], ALU.subtract, ALU.mult)
                a.then_inc(normed_ready, 1)

            def expert_step(g):
                if g.within(GROUPS):
                    experts = load_experts(dve, registers, g.number)
                if g.ahead(-1).within(GROUPS):
                    norm_rows(g.ahead(-1))
                if g.within(GROUPS):
                    hidden_rows(g, experts)

            per_step = 3 * CHUNK + 6
            walk_groups(dve, GROUPS, expert_step, 0, 1,
                        enter=lambda i: chain.enter(4 * per_step, i), leave=chain.leave)

            def final_statistics(k, c):
                dve.wait_ge(pair_mixed, k + 1)
                wait(dve, final_ready, k - 1)
                residual = x1_all[:, bass.ds(k, 1), :, :].rearrange("p a t d -> p (a t) d")
                then(dve.tensor_tensor(total_row[c][:], mixed[c][:], residual, ALU.add))
                sync()
                for t in range(CHUNK):
                    then(dve.bn_stats(stats[:, c, t, :], total_row[c][:, t, :]))
                sync()
                hold()
                for t in range(CHUNK):
                    then(dve.bn_aggr(mean_var[:, c, t, :], stats[:, c, t, :]))
                sync()
                then(dve.tensor_scalar(minus_mean[:, c, :], mean_var[:, c, :, 0], -1.0, None, ALU.mult))
                dve.tensor_scalar(var[:, c, :], mean_var[:, c, :, 1], EPS, None, ALU.add).then_inc(fv_ready, 1)

            for c in range(2):
                final_statistics(c, c)
            with dve.Fori(0, NB - 1) as i:
                chain.enter(2 * (2 * CHUNK + 2), i)
                for c in range(2):
                    final_statistics(2 * i + 2 + c, c)
            chain.leave(NB - 1)


_INS = ["L0_attn_x", "L0_attn_w_q", "L0_attn_b_q", "L0_attn_w_k", "L0_attn_b_k", "L0_attn_w_v", "L0_attn_b_v",
        "L0_attn_w_out", "L0_attn_b_out", "L0_ffn_Wr", "L0_ffn_br", "L0_ffn_W1", "L0_ffn_b1", "L0_ffn_g1",
        "L0_ffn_be1", "L0_ffn_W2", "L0_ffn_b2"]


def kernel(**inputs):
    import numpy as _np
    import concourse.bacc as _bacc
    from concourse import mybir as _mybir
    from concourse.bass_utils import run_bass_kernel_spmd as _run

    nc = _bacc.Bacc("TRN2", target_bir_lowering=False, num_devices=1)
    arrays, args = {}, []
    for name in _INS:
        a = _np.ascontiguousarray(inputs[name])
        arrays[f"in_{name}_dram"] = a
        args.append(nc.dram_tensor(f"in_{name}_dram", a.shape, _mybir.dt.from_np(a.dtype), kind="ExternalInput").ap())
    shape = inputs["L0_attn_x"].shape
    out = nc.dram_tensor("out_0_dram", shape, _mybir.dt.float32, kind="ExternalOutput").ap()
    post_ln_moe_layer(nc, *args, out)
    r = _run(nc, [arrays], core_ids=[0])
    return r.results[0]["out_0_dram"]
```

```python
from contextlib import ExitStack

import concourse.bass as bass
from concourse import mybir

F32 = mybir.dt.float32
F32R = mybir.dt.float32r
BF16 = mybir.dt.bfloat16
I32 = mybir.dt.int32
U32 = mybir.dt.uint32
ALU = mybir.AluOpType
ACT = mybir.ActivationFunctionType
AX = mybir.AxisListType

P = 128
EPS = 1e-5


def wait(engine, sem, value):
    if isinstance(value, int) and value <= 0:
        return
    engine.wait_ge(sem, value)


class Chain:

    def __init__(self, engine, sem):
        self.engine, self.sem, self.base, self.steps = engine, sem, 0, 0

    def then(self, instruction):
        instruction.then_inc(self.sem, 1)
        self.steps += 1

    def sync(self, behind=0):
        wait(self.engine, self.sem, self.base + self.steps - behind)

    def enter(self, per_iteration, i):
        self.outer, self.per = self.base + self.steps, per_iteration
        self.base, self.steps = self.outer + i * per_iteration, 0

    def leave(self, iterations):
        assert self.steps == self.per, self.steps
        self.base, self.steps = self.outer + iterations * self.per, 0


class Group:

    def __init__(self, number, fours, quarter):
        self.number, self.fours, self.quarter = number, fours, quarter
        self.parity, self.pairs = quarter % 2, 2 * fours + quarter // 2

    def ahead(self, d):
        q = self.quarter + d
        return Group(self.number + d, self.fours + q // 4, q % 4)

    def within(self, groups):
        return not isinstance(self.number, int) or 0 <= self.number < groups


def walk_groups(engine, groups, step, lead, tail, enter=None, leave=None):
    for s in range(-lead, 4):
        step(Group(s, s // 4, s % 4))
    fours = groups // 4 - 2
    with engine.Fori(0, fours) as i:
        if enter:
            enter(i)
        for q in range(4):
            step(Group(4 * i + 4 + q, i + 1, q))
    if leave:
        leave(fours)
    for s in range(groups - 4, groups + tail):
        step(Group(s, s // 4, s % 4))


def post_ln_moe_layer(nc, x, w_q, b_q, w_k, b_k, w_v, b_v, w_out, b_out,
                      w_r, b_r, w_1, b_1, g_1, be_1, w_2, b_2, out):
    NB, S, D = x.shape
    E = w_r.shape[1]
    H = w_1.shape[2]
    N = NB * S
    TILES = S // P
    CHUNK = 4
    CHUNKS = NB * TILES // CHUNK
    CW = CHUNK * P
    KT = S // P
    KH = KT // 2
    SPLIT = (1,)
    assert D == P and H == P and TILES == 2 * CHUNK and NB % 2 == 0
    SCALE = float(D) ** -0.5
    REGION = N + P
    ROW = D + 4
    EXPERT_TILES = -(-(2 * N // P + E) // CHUNK) * CHUNK
    GROUPS = EXPERT_TILES // CHUNK
    assert GROUPS % 4 == 0 and GROUPS >= 12 and EXPERT_TILES <= 2 * P

    with ExitStack() as ctx, ExitStack() as late:
        def sb(name, shape, dt=F32, stack=None):
            return (stack or ctx).enter_context(nc.sbuf_tensor(name, shape, dt))

        def sem(name):
            return ctx.enter_context(nc.semaphore(name))

        routed = nc.dram_tensor("routed_rows", [E * REGION, ROW], F32).ap()
        chosen = nc.dram_tensor("expert_rows", [2 * N, D], F32).ap()

        x_v = x.rearrange("n (p j) d -> n p j d", p=P)
        out_v = out.rearrange("n (p c j) d -> n c p j d", p=P, c=2)
        chosen_v = chosen.rearrange("(n p c j k) d -> n c p j k d", n=NB, p=P, c=2, k=2)

        ident = sb("ident", [P, P])
        partition = sb("partition", [P, 1])
        column = sb("column", [P, P])
        expert_ids = sb("expert_ids", [P, E])
        b2_row = sb("b2_row", [1, E, D])
        ones = sb("ones", [P, P])
        x1_all = sb("x1_all", [P, CHUNKS, CHUNK, D])
        g_rows = sb("g_rows", [E, 2, H])
        g_cols = sb("g_cols", [P, 2, E])
        minus_half = sb("minus_half", [P, CHUNK])
        region_start = sb("region_start", [P, E])
        pad_row = sb("pad_row", [P, ROW])
        base = sb("base", [P, 2, E])
        base_i = sb("base_i", [P, E], I32)
        tile_table = sb("tile_table", [1, 4 * P], I32)
        var = sb("var", [P, 2, CHUNK])
        minus_mean = sb("minus_mean", [P, 2, CHUNK])
        shift = sb("shift", [P, 4, CHUNK])
        rstd = sb("rstd", [P, 4, CHUNK])
        stats = sb("stats", [P, 2, CHUNK, 6])
        mean_var = sb("mean_var", [P, 2, CHUNK, 2])
        tab = sb("tab", [P, 8, E])
        tab_i = sb("tab_i", [P, E], I32)
        per_tile = sb("per_tile", [P, 2, E])
        per_tile2 = sb("per_tile2", [P, 2, E])
        tile_cols = sb("tile_cols", [P, 4])
        expert_cols = sb("expert_cols", [P, 2, P])
        expert_of_tile = sb("expert_of_tile", [P, 2 * P])

        with ExitStack() as early:
            def sb1(name, shape, dt=F32):
                return sb(name, shape, dt, early)

            qkT_hi = [[sb1(f"{n}T_hi{i}", [P, S], F32R) for n in "qk"] for i in range(2)]
            qkT_lo = [[sb1(f"{n}T_lo{i}", [P, S], F32R) for n in "qk"] for i in range(2)]
            w_rows = [sb1(f"w_rows{i}", [P, D]) for i in range(4)]
            wT = sb1("wT", [P, 2, D])
            woutT = sb1("woutT", [P, D])
            wvo = sb1("wvo", [P, D])
            bq = sb1("bq", [P, 1])
            bk = sb1("bk", [P, 1])
            bv = sb1("bv", [P, 1])
            bv_cols = sb1("bv_cols", [P, P])
            bout_bc = sb1("bout_bc", [P, D])
            bvo_bc = sb1("bvo_bc", [P, D])
            wr_sb = sb1("wr_sb", [P, E])
            br_bc = sb1("br_bc", [P, E])
            iota_i = sb1("iota_i", [P, P + 1], I32)
            before = sb1("before", [P, P], BF16)
            ones_h = sb1("ones_h", [P, P], BF16)
            row_ids = sb1("row_ids", [P, 2, CHUNK])

            x_tok = [sb1(f"x_tok{i}", [P, TILES, D]) for i in range(2)]
            xT = sb1("xT", [P, S])
            v_sum = sb1("v_sum", [P, KH, D])
            v, v_lo, pT, pT_lo = {}, {}, {}, {}
            for i in range(2):
                for h in range(2):
                    dt = F32R if h in SPLIT else F32
                    v[i, h] = sb1(f"v{i}_{h}", [P, KH, D], dt)
                    pT[i, h] = sb1(f"pT{i}_{h}", [P, KH, CW], dt)
                    if h in SPLIT:
                        v_lo[i, h] = sb1(f"v_lo{i}_{h}", [P, KH, D], dt)
                        pT_lo[i, h] = sb1(f"pT_lo{i}_{h}", [P, KH, CW], dt)
            minus_max = sb1("minus_max", [P, 2])
            probs = [sb1(f"probs{i}", [P, S]) for i in range(2)]
            total = sb1("total", [P, 2 * TILES])
            inv_total = sb1("inv_total", [P, CHUNK])
            attnT = sb1("attnT", [P, CW])
            x_res = [sb1(f"x_res{i}", [P, CHUNK, D]) for i in range(2)]
            summed = sb1("summed", [P, CHUNK, D])
            x1 = [sb1(f"x1_{i}", [P, CHUNK, ROW]) for i in range(3)]
            x1T = sb1("x1T", [P, CW])
            logits = sb1("logits", [P, CHUNK, E])
            top = sb1("top", [P, CHUNK, 8])
            top_i = sb1("top_i", [P, CHUNK, 8], U32)
            top_f = sb1("top_f", [P, CHUNK, 2])
            picked = sb1("picked", [P, 2, CHUNK, E])
            picked_h = sb1("picked_h", [P, CHUNK + 1, E], BF16)
            shifted = sb1("shifted", [P, CHUNK, E + 2])
            expd = sb1("expd", [P, CHUNK, E + 2])
            gate_sum = sb1("gate_sum", [P, 4, CHUNK])
            gate_p = sb1("gate_p", [P, CHUNK, 2])
            rank = sb1("rank", [P, CHUNK, E])
            rank_k = sb1("rank_k", [P, 2, CHUNK, E])
            place_f = sb1("place_f", [P, 2, CHUNK])
            place = [sb1(f"place{i}", [P, 2, CHUNK], U32) for i in range(3)]

        def sb2(name, shape, dt=F32):
            return sb(name, shape, dt, late)

        w1_sb = sb2("w1_sb", [P, E, H])
        w2_sb = sb2("w2_sb", [P, E, D])
        b1_bc = sb2("b1_bc", [P, E, H])
        assert (2 * H + D) * E <= 8 * S
        row_in = [sb2(f"row_in{i}", [P, CHUNK, ROW]) for i in range(4)]
        inT = [sb2(f"inT{i}", [P, CW]) for i in range(2)]
        hidden = [sb2(f"hidden{i}", [P, CHUNK, H]) for i in range(2)]
        normed = [sb2(f"normed{i}", [P, CHUNK, H]) for i in range(2)]
        actT = [sb2(f"actT{i}", [P, CW]) for i in range(2)]
        row_out = [sb2(f"row_out{i}", [P, CHUNK, D]) for i in range(2)]
        is_second = sb2("is_second", [P, CHUNK])
        dest_f = sb2("dest_f", [P, CHUNK])
        gate_part = sb2("gate_part", [P, 3, CHUNK])
        dest = [sb2(f"dest{i}", [P, CHUNK], U32) for i in range(4)]
        gate = [sb2(f"gate{i}", [P, CHUNK]) for i in range(4)]
        pair = [sb2(f"pair{i}", [P, CHUNK, 2, D]) for i in range(4)]
        mixed = [sb2(f"mixed{i}", [P, CHUNK, D]) for i in range(2)]
        final = [sb2(f"final{i}", [P, CHUNK, D]) for i in range(4)]

        scores = [ctx.enter_context(nc.psum_tensor(f"scores{i}", [P, 2, 512], F32)) for i in range(2)]
        turned = ctx.enter_context(nc.psum_tensor("turned", [P, 2, 512], F32))
        value_sum = ctx.enter_context(nc.psum_tensor("value_sum", [P, 512], F32))
        work = ctx.enter_context(nc.psum_tensor("work", [P, 512], F32))

        (weights_in, consts_in, expert_in, gains_in, iota_done, ident_ready, setup_pe, setup_dve,
         proj_filled, proj_split, proj_taken, scores_ready, max_ready, probs_ready, turned_ready,
         v_hi_ready, v_ready, values_ready, attnT_copied, attn_ready, attn_taken,
         var_ready, rstd_ready, x1_ready, x1_turned, x1T_ready, logits_ready, logits_taken,
         mask_ready, exp_ready, rank_ready, rank_taken, place_ready, pad_ready, pad_in,
         table_pe, table_ready, pool_const, cols_ready) = [sem(n) for n in (
             "weights_in consts_in expert_in gains_in iota_done ident_ready setup_pe setup_dve "
             "proj_filled proj_split proj_taken scores_ready max_ready probs_ready turned_ready "
             "v_hi_ready v_ready values_ready attnT_copied attn_ready attn_taken "
             "var_ready rstd_ready x1_ready x1_turned x1T_ready logits_ready logits_taken "
             "mask_ready exp_ready rank_ready rank_taken place_ready pad_ready pad_in "
             "table_pe table_ready pool_const cols_ready").split()]
        pT_hi_ready = [sem(f"pT_hi_ready{h}") for h in range(2)]
        pT_ready = [sem(f"pT_ready{h}") for h in range(2)]
        x_in = [sem(f"x_in{i}") for i in range(2)]
        res_in = [sem(f"res_in{i}") for i in range(2)]
        scattered = [sem(f"scattered{i}") for i in range(2)]
        x1_kept = sem("x1_kept")
        rows_in = [sem(f"rows_in{i}") for i in range(4)]
        (in_turned, inT_ready, hidden_ready, hidden_var_ready, hidden_scale_ready, normed_ready, norm_turned,
         actT_ready, result_ready) = [sem(n) for n in (
             "in_turned inT_ready hidden_ready hidden_var_ready hidden_scale_ready normed_ready norm_turned "
             "actT_ready result_ready").split()]
        result_taken, gate_ready = sem("result_taken"), sem("gate_ready")
        delivered = [sem(f"delivered{i}") for i in range(2)]
        pair_in = [sem(f"pair_in{i}") for i in range(4)]
        (pair_mixed, row_total, final_var_ready, final_scale_ready, shift_ready, final_ready) = [
            sem(n) for n in (
                "pair_mixed row_total final_var_ready final_scale_ready shift_ready final_ready").split()]
        final_out = [sem(f"final_out{i}") for i in range(4)]
        dve_chain, dve_held, pool_held = sem("dve_chain"), sem("dve_held"), sem("pool_held")

        def split(h):
            return h in SPLIT

        BATCH_LOOPS = (NB - 4) // 2

        def projection_bank(n, j):
            if isinstance(n, int) and n == 0:
                return (turned[:, 0, :], turned[:, 1, :], scores[0][:, 0, :], scores[0][:, 1, :],
                        scores[1][:, 0, :], scores[1][:, 1, :])[j % 6]
            return work[:]

        def routing_bank(C):
            last = isinstance(C, int) and C == CHUNKS - 1
            return scores[0][:, 0, :] if last else work[:]

        def rows_buffer(C, c):
            return 2 if isinstance(C, int) and C == CHUNKS - 1 else c

        def live(chunk):
            return not isinstance(chunk, int) or chunk >= 0

        def walk_chunks(engine, step, enter=None, leave=None):
            for k in range(8):
                step(k, k // 4, k % 4)
            with engine.Fori(0, CHUNKS // 4 - 2) as i:
                if enter:
                    enter(i)
                for q in range(4):
                    step(4 * i + 8 + q, i + 2, q)
            if leave:
                leave(CHUNKS // 4 - 2)

        def expert_registers(engine, name, groups):
            return [engine.alloc_register(f"{name}{i}") for i in range(CHUNK * groups)]

        def load_experts(engine, registers, group):
            n = len(registers)
            engine.load(registers, tile_table[0:1, bass.ds(group * CHUNK, n)])
            return [engine.snap(r, min_val=0, max_val=E - 1) for r in registers]

        block = ctx.enter_context(nc.Block())

        @block.sync
        def _(sp):
            for i, w in enumerate((w_q, w_k, w_v, w_out)):
                sp.dma_start(w_rows[i][:], w).then_inc(weights_in, 16)
            sp.dma_start(x_tok[0][:], x_v[0]).then_inc(x_in[0], 16)
            for dst, b in ((bq, b_q), (bk, b_k), (bv, b_v)):
                sp.dma_start(dst[:], b.rearrange("(d a) -> d a", a=1)).then_inc(consts_in, 16)
            sp.dma_start(bout_bc[:], b_out.rearrange("(a d) -> a d", a=1).to_broadcast([P, D])).then_inc(consts_in, 16)
            sp.dma_start(wr_sb[:], w_r).then_inc(consts_in, 16)
            sp.dma_start(br_bc[:], b_r.rearrange("(a d) -> a d", a=1).to_broadcast([P, E])).then_inc(consts_in, 16)
            sp.dma_start(g_rows[:, 0, :], g_1).then_inc(gains_in, 16)
            sp.dma_start(g_rows[:, 1, :], be_1).then_inc(gains_in, 16)
            sp.dma_start(x_tok[1][:], x_v[1]).then_inc(x_in[1], 16)
            sp.dma_start(b2_row[:], b_2.rearrange("(a e) h -> a e h", a=1)).then_inc(expert_in, 16)

            def batch(n, p, load=True):
                for c in range(2):
                    wait(sp, attn_taken, 2 * n + c - 1)
                    sp.dma_start(x_res[c][:], x_v[n][:, CHUNK * c:CHUNK * (c + 1), :]).then_inc(res_in[c], 16)
                if load:
                    wait(sp, proj_filled, 8 * n + 2)
                    sp.dma_start(x_tok[p][:], x_v[n + 2]).then_inc(x_in[p], 16)

            batch(0, 0)
            with sp.Fori(0, BATCH_LOOPS) as i:
                batch(2 * i + 1, 1)
                batch(2 * i + 2, 0)
            batch(NB - 3, 1)
            batch(NB - 2, 0, load=False)
            batch(NB - 1, 1, load=False)

            sp.wait_ge(scores_ready, NB * TILES)
            sp.dma_start(w1_sb[:], w_1.rearrange("e i h -> i e h")).then_inc(expert_in, 16)
            sp.dma_start(w2_sb[:], w_2.rearrange("e i h -> i e h")).then_inc(expert_in, 16)
            sp.dma_start(b1_bc[:], b_1.rearrange("(a e) h -> a e h", a=1).to_broadcast([P, E, H])).then_inc(expert_in, 16)

            ends = [sp.alloc_register(f"end{i}") for i in range(4)]
            sp.wait_ge(pad_ready, 1)
            for e0 in range(0, E, 4):
                sp.load(ends, base_i[0:1, e0:e0 + 4])
                for i, r in enumerate(ends):
                    e = e0 + i
                    start = sp.snap(r, min_val=e * REGION, max_val=e * REGION + N)
                    sp.dma_start(routed[bass.ds(start, P), :], pad_row[:]).then_inc(pad_in, 16)
            sp.wait_ge(table_ready, 1)
            row_registers = [sp.alloc_register(f"row{i}") for i in range(CHUNK)]

            def rows(g):
                if not g.within(GROUPS):
                    return
                sp.load(row_registers, tile_table[0:1, bass.ds(g.number * CHUNK + 2 * P, CHUNK)])
                if isinstance(g.number, int) and g.number == 0:
                    sp.wait_ge(pad_in, 16 * E)
                    for c in range(2):
                        sp.wait_ge(scattered[c], 16 * 2 * CHUNK * (CHUNKS // 2))
                wait(sp, in_turned, g.number - 3)
                wait(sp, hidden_var_ready, g.number - 3)
                for t, r in enumerate(row_registers):
                    row = sp.snap(r, min_val=0, max_val=E * REGION - P)
                    sp.dma_start(row_in[g.quarter][:, t, :],
                                 routed[bass.ds(row, P), :]).then_inc(rows_in[g.quarter], 16)

            walk_groups(sp, GROUPS, rows, 0, 0)

            for p in range(2):
                sp.wait_ge(delivered[p], 16 * CHUNK * (GROUPS // 2))

            def pair_rows(k, fours, q):
                wait(sp, pair_mixed, k - 3)
                sp.dma_start(pair[q][:], chosen_v[2 * fours + q // 2][q % 2]).then_inc(pair_in[q], 16)

            walk_chunks(sp, pair_rows)
            for q in range(4):
                sp.wait_ge(final_out[q], 16 * CHUNKS // 4)

        @block.gpsimd
        def _(pool):
            def hold():
                pool.sem_inc(pool_held, 1)

            pool.iota(iota_i[:, 0:P], [[1, P]], base=0, channel_multiplier=0).then_inc(iota_done, 1)
            pool.iota(iota_i[:, P:P + 1], [[1, 1]], base=0, channel_multiplier=1).then_inc(iota_done, 1)
            pool.memset(minus_half[:], -0.5).then_inc(pool_const, 1)
            pool.memset(ones_h[:], 1.0).then_inc(pool_const, 1)
            pool.memset(pad_row[:], 0.0).then_inc(pool_const, 1)
            pool.wait_ge(pool_const, 3)

            def scale(C):
                pool.wait_ge(var_ready, C + 1)
                pool.tensor_tensor(rstd[:, 0, :], var[:, 0, :], minus_half[:], ALU.pow).then_inc(rstd_ready, 1)
                pool.wait_ge(rstd_ready, 2 * C + 1)
                pool.tensor_tensor(shift[:, 0, :], minus_mean[:, 0, :], rstd[:, 0, :], ALU.mult).then_inc(rstd_ready, 1)

            def keep(C, c):
                pool.wait_ge(x1_ready, C + 1)
                pool.tensor_copy(x1_all[:, bass.ds(C, 1), :, :].rearrange("p a t d -> p (a t) d"),
                                 x1[rows_buffer(C, c)][:, :, 0:D]).then_inc(x1_kept, 1)

            def scatter(C, c, tiles=range(CHUNK)):
                pool.wait_ge(place_ready, C + 1)
                hold()
                for t in tiles:
                    for s in range(2):
                        pool.indirect_dma_start(
                            routed, bass.IndirectOffsetOnAxis(ap=place[rows_buffer(C, c)][:, s, t:t + 1], axis=0),
                            x1[rows_buffer(C, c)][:, t, :], None).then_inc(scattered[c], 16)

            scale(0)
            keep(0, 0)
            with pool.Fori(0, CHUNKS // 2 - 2) as i:
                for c in range(2):
                    scale(2 * i + c + 1)
                    keep(2 * i + c + 1, 1 - c)
                    scatter(2 * i + c, c)
            B, A = CHUNKS - 2, CHUNKS - 1
            scale(B - 1)
            keep(B - 1, 1)
            scatter(B - 2, 0)
            scale(B)
            scatter(B - 1, 1, range(0, CHUNK // 2))
            scale(A)
            scatter(B - 1, 1, range(CHUNK // 2, CHUNK))
            scatter(B, 0)
            scatter(A, 1)
            keep(B, 0)
            keep(A, 1)

            def expert_step(g):
                if g.within(GROUPS):
                    pool.wait_ge(hidden_var_ready, g.number + 1)
                    wait(pool, normed_ready, g.number - 1)
                    pool.tensor_tensor(rstd[:, g.parity, :], var[:, g.parity, :], minus_half[:],
                                       ALU.pow).then_inc(hidden_scale_ready, 1)
                g = g.ahead(-2)
                if g.within(GROUPS):
                    pool.wait_ge(result_taken, g.number + 1)
                    hold()
                    for t in range(CHUNK):
                        pool.indirect_dma_start(
                            chosen, bass.IndirectOffsetOnAxis(ap=dest[g.quarter][:, t:t + 1], axis=0),
                            row_out[g.parity][:, t, :], None, bounds_check=2 * N - 1,
                            oob_is_err=False).then_inc(delivered[g.parity], 16)

            walk_groups(pool, GROUPS, expert_step, 0, 2)

            def final_scale(k, q):
                pool.wait_ge(final_var_ready, k + 1)
                wait(pool, final_ready, k - 3)
                pool.tensor_tensor(rstd[:, q, :], var[:, q % 2, :], minus_half[:], ALU.pow).then_inc(final_scale_ready, 1)

            def mix(k, fours, q):
                pool.wait_ge(pair_in[q], 16 * (fours + 1))
                wait(pool, row_total, k - 1)
                pool.tensor_tensor(mixed[q % 2][:], pair[q][:, :, 0, :], pair[q][:, :, 1, :],
                                   ALU.add).then_inc(pair_mixed, 1)
                if not isinstance(k, int) or k >= 2:
                    final_scale(k - 2, (q - 2) % 4)

            walk_chunks(pool, mix)
            for k in (CHUNKS - 2, CHUNKS - 1):
                final_scale(k, k % 4)

        @block.tensor
        def _(pe):
            pe.wait_ge(weights_in, 64)
            pe.wait_ge(ident_ready, 1)
            for i, src in enumerate((0, 1, 3)):
                mm = pe.transpose(work[:, i * P:(i + 1) * P], w_rows[src][:], ident[:])
            mm.then_inc(setup_pe, 1)

            def values_setup():
                pe.wait_ge(setup_dve, 2)
                pe.matmul(value_sum[:, 0:D], w_rows[2][:], woutT[:], start=True, stop=True)
                pe.matmul(value_sum[:, D:2 * D], bv_cols[:], woutT[:], start=True, stop=True)
                pe.wait_ge(gains_in, 32)
                for i in range(2):
                    mm = pe.transpose(value_sum[:, 2 * D + i * E:2 * D + (i + 1) * E], g_rows[:, i, :],
                                      ident[0:E, 0:E])
                mm.then_inc(setup_pe, 1)
                pe.wait_ge(setup_dve, 5)

            def three_passes(dst, a_hi, a_lo, b_hi, b_lo, start=True, stop=True):
                pe.matmul(dst, a_hi, b_hi, start=start, stop=False)
                pe.matmul(dst, a_hi, b_lo, start=False, stop=False)
                return pe.matmul(dst, a_lo, b_hi, start=False, stop=stop)

            def project(n, m, p, j):
                bank = projection_bank(n, j)
                h = j % 2
                cols = slice(h * CW, (h + 1) * CW)
                if j < 2:
                    pe.wait_ge(x_in[p], 16 * (m + 1))
                    for t in range(CHUNK):
                        mm = pe.transpose(bank[:, t * P:(t + 1) * P], x_tok[p][:, h * CHUNK + t, :], ident[:])
                elif j < 6:
                    k = (j - 2) // 2
                    pe.wait_ge(proj_taken, 8 * n + 2)
                    if isinstance(n, int) and n == 0:
                        pe.wait_ge(setup_dve, 1)
                    mm = pe.matmul(bank[:], wT[:, k, :], xT[:, cols], start=True, stop=True)
                else:
                    for t in range(CHUNK):
                        mm = pe.matmul(bank[:, t * D:(t + 1) * D],
                                       xT[:, h * CW + t * P:h * CW + (t + 1) * P], wvo[:], start=True, stop=True)
                mm.then_inc(proj_filled, 1)

            def score(s, p, j):
                wait(pe, probs_ready, s - 1)
                q = slice(j * P, (j + 1) * P)
                for h in range(2):
                    k = slice(h * CW, (h + 1) * CW)
                    mm = three_passes(scores[j % 2][:, h, :], qkT_hi[p][0][:, q], qkT_lo[p][0][:, q],
                                      qkT_hi[p][1][:, k], qkT_lo[p][1][:, k])
                mm.then_inc(scores_ready, 1)

            def turn(s, j):
                pe.wait_ge(probs_ready, s + 1)
                for h in range(2):
                    wait(pe, pT_ready[h], s)
                    for t in range(4):
                        k = 4 * h + t
                        mm = pe.transpose(turned[:, h, t * P:(t + 1) * P],
                                          probs[j % 2][:, k * P:(k + 1) * P], ident[:])
                    mm.then_inc(turned_ready, 1)

            def weigh(C, c, vp, r):
                if r == 0:
                    for h in range(2):
                        pe.wait_ge(pT_ready[h], CHUNK * (C + 1))
                    wait(pe, attnT_copied, C)
                for k in (2 * r, 2 * r + 1):
                    h, i = k // KH, k % KH
                    ends = dict(start=(k == 0), stop=(k == KT - 1))
                    if split(h):
                        mm = three_passes(value_sum[:], v[vp, h][:, i, :], v_lo[vp, h][:, i, :],
                                          pT[c, h][:, i, :], pT_lo[c, h][:, i, :], **ends)
                    else:
                        mm = pe.matmul(value_sum[:], v[vp, h][:, i, :], pT[c, h][:, i, :], **ends)
                if r == 3:
                    mm.then_inc(values_ready, 1)

            def turn_back(C):
                bank = routing_bank(C)
                pe.wait_ge(attnT_copied, C + 1)
                for t in range(CHUNK):
                    mm = pe.transpose(bank[:, t * P:(t + 1) * P], attnT[:, t * P:(t + 1) * P], ident[:])
                mm.then_inc(attn_ready, 1)

            def turn_x1(C, c):
                bank = routing_bank(C)
                pe.wait_ge(x1_ready, C + 1)
                for t in range(CHUNK):
                    mm = pe.transpose(bank[:, t * P:(t + 1) * P], x1[rows_buffer(C, c)][:, t, 0:D], ident[:])
                mm.then_inc(x1_turned, 1)

            def router(C):
                bank = routing_bank(C)
                pe.wait_ge(x1T_ready, C + 1)
                for t in range(CHUNK):
                    mm = pe.matmul(bank[:, t * E:(t + 1) * E], x1T[:, t * P:(t + 1) * P], wr_sb[:],
                                   start=True, stop=True)
                mm.then_inc(logits_ready, 1)

            def rank_picks(C):
                bank = routing_bank(C)
                pe.wait_ge(mask_ready, C + 1)
                pe.matmul(bank[:, 0:(CHUNK + 1) * E], before[:], picked_h[:].rearrange("p t e -> p (t e)"),
                          start=True, stop=False)
                for t in range(CHUNK):
                    after = CHUNK - t
                    mm = pe.matmul(bank[:, (t + 1) * E:(CHUNK + 1) * E].rearrange("p (t e) -> p t e", t=after),
                                   ones_h[:], picked_h[:, t:t + 1, :].to_broadcast([P, after, E]),
                                   start=False, stop=(t == CHUNK - 1))
                mm.then_inc(rank_ready, 1)

            def route(C, c, r):
                if r == 0 and live(C - 2):
                    turn_back(C - 2)
                if r == 1 and live(C - 3):
                    rank_picks(C - 3)
                if r == 2 and live(C - 2):
                    turn_x1(C - 2, c)
                if r == 3 and live(C - 2):
                    router(C - 2)

            def work_free(C, r):
                if r == 0:
                    wait(pe, logits_taken, C - 2)
                if r == 1:
                    wait(pe, attn_taken, C - 1)
                if r == 2:
                    wait(pe, rank_taken, C - 2)
                if r == 3:
                    wait(pe, x1T_ready, C - 1)

            def batch(n, m, p, score_next=True, project_next=True):
                for j in range(TILES):
                    c, r = j // CHUNK, j % CHUNK
                    s, C = TILES * n + j, 2 * n + c
                    if j < TILES - 1:
                        score(s + 1, p, j + 1)
                    elif score_next:
                        pe.wait_ge(proj_taken, 8 * (n + 1) + 6)
                        score(s + 1, 1 - p, 0)
                    if r == 1:
                        turn(s, j)
                    if project_next:
                        if isinstance(n, int):
                            pe.wait_ge(proj_taken, 8 * (n + 1) + j)
                        work_free(C, r)
                        project(n + 1, m + p, 1 - p, j)
                    if r != 1:
                        turn(s, j)
                    if live(C - 1):
                        if r == 0 and c == 1:
                            pe.wait_ge(proj_taken, 8 * (n + 1))
                            pe.wait_ge(v_ready, len(SPLIT) * (n + 1))
                        weigh(C - 1, 1 - c, (1 - p) if c == 0 else p, r)
                    if project_next:
                        if live(C - 2):
                            pe.wait_ge(proj_taken, 8 * (n + 1) + j + 1)
                    else:
                        work_free(C, r)
                    route(C, c, r)

            for j in range(TILES):
                if j == 6:
                    values_setup()
                project(0, 0, 0, j)
            pe.wait_ge(proj_taken, 6)
            score(0, 0, 0)
            pe.wait_ge(proj_taken, 8)
            batch(0, 0, 0)
            batch(1, 0, 1)
            with pe.Fori(0, BATCH_LOOPS) as i:
                batch(2 * i + 2, i + 1, 0)
                batch(2 * i + 3, i + 1, 1)
            batch(NB - 2, NB // 2 - 1, 0)
            batch(NB - 1, NB // 2 - 1, 1, score_next=False, project_next=False)
            B, A = CHUNKS - 2, CHUNKS - 1
            pe.wait_ge(logits_taken, B)
            turn_back(B)
            weigh(A, 1, 1, 0)
            weigh(A, 1, 1, 1)
            pe.wait_ge(attn_taken, B + 1)
            rank_picks(B - 1)
            weigh(A, 1, 1, 2)
            weigh(A, 1, 1, 3)
            turn_back(A)
            pe.wait_ge(rank_taken, B)
            turn_x1(B, 0)
            router(B)
            pe.wait_ge(attn_taken, A + 1)
            turn_x1(A, 1)
            pe.wait_ge(logits_taken, B + 1)
            rank_picks(B)
            router(A)
            pe.wait_ge(logits_taken, A + 1)
            rank_picks(A)
            pe.wait_ge(rank_taken, A + 1)

            pe.wait_ge(cols_ready, 2)
            for i in range(4):
                mm = pe.matmul(work[0:1, i * P:(i + 1) * P], tile_cols[:, i:i + 1], ident[:], start=True, stop=True)
            mm.then_inc(table_pe, 1)
            pe.wait_ge(cols_ready, 4)
            for i in range(2):
                mm = pe.matmul(value_sum[:, i * P:(i + 1) * P], expert_cols[:, i, :], ident[:], start=True, stop=True)
            mm.then_inc(table_pe, 1)
            pe.wait_ge(table_ready, 1)
            pe.wait_ge(expert_in, 64)
            registers = expert_registers(pe, "expert", 3)

            def turn_rows(g):
                pe.wait_ge(rows_in[g.quarter], 16 * CHUNK * (g.fours + 1))
                wait(pe, inT_ready, g.number - 1)
                for t in range(CHUNK):
                    mm = pe.transpose(scores[g.parity][:, 0, t * P:(t + 1) * P], row_in[g.quarter][:, t, 0:D], ident[:])
                mm.then_inc(in_turned, 1)

            def first_product(g, experts):
                p = g.parity
                pe.wait_ge(inT_ready, g.number + 1)
                wait(pe, hidden_var_ready, g.number - 1)
                for t in range(CHUNK):
                    mm = pe.matmul(scores[p][:, 1, t * H:(t + 1) * H], inT[p][:, t * P:(t + 1) * P],
                                   w1_sb[:, bass.ds(experts[t], 1), :], start=True, stop=True)
                mm.then_inc(hidden_ready, 1)

            def turn_hidden(g):
                p = g.parity
                pe.wait_ge(normed_ready, g.number + 1)
                for t in range(CHUNK):
                    mm = pe.transpose(turned[:, p, t * P:(t + 1) * P], normed[p][:, t, :], ident[:])
                mm.then_inc(norm_turned, 1)

            def second_bias(g, experts):
                wait(pe, result_taken, g.number - 1)
                dst = (value_sum, work)[g.parity]
                for t in range(CHUNK):
                    pe.matmul(dst[:, t * D:(t + 1) * D], ones[0:1, :], b2_row[0:1, bass.ds(experts[t], 1), :],
                              start=(t == 0), stop=False)

            def second_product(g, experts):
                pe.wait_ge(actT_ready, g.number + 1)
                dst = (value_sum, work)[g.parity]
                for t in range(CHUNK):
                    mm = pe.matmul(dst[:, t * D:(t + 1) * D], actT[g.parity][:, t * P:(t + 1) * P],
                                   w2_sb[:, bass.ds(experts[t], 1), :], start=False, stop=(t == CHUNK - 1))
                mm.then_inc(result_ready, 1)

            def expert_step(g):
                last, after = g.ahead(-1), g.ahead(1)
                if isinstance(g.number, int):
                    start = min(max(last.number, 0), GROUPS - 3)
                    skip = last.number - start
                else:
                    start, skip = last.number, 0
                experts = load_experts(pe, registers, start)
                if last.within(GROUPS):
                    experts_last = experts[CHUNK * skip:]
                if after.within(GROUPS):
                    experts_after = experts[CHUNK * (skip + 2):]
                if last.within(GROUPS):
                    turn_hidden(last)
                    second_bias(last, experts_last)
                if after.within(GROUPS):
                    first_product(after, experts_after)
                if g.ahead(2).within(GROUPS):
                    turn_rows(g.ahead(2))
                if last.within(GROUPS):
                    second_product(last, experts_last)

            walk_groups(pe, GROUPS, expert_step, 2, 1)

        @block.scalar
        def _(act):
            act.preload_act_table(ACT.Exp)
            def project(n, p, j):
                h, bank = j % 2, projection_bank(n, j)
                cols = slice(h * CW, (h + 1) * CW)
                if j < 6:
                    act.wait_ge(proj_filled, 8 * n + j + 1)
                if j < 2:
                    act.copy(xT[:, cols], bank[:]).then_inc(proj_taken, 1)
                elif j < 6:
                    k = (j - 2) // 2
                    if isinstance(n, int) and n == 0:
                        act.wait_ge(setup_dve, 2)
                    act.activation(qkT_hi[p][k][:, cols], bank[:], ACT.Identity,
                                   bias=(bq, bk)[k][:, 0:1]).then_inc(proj_split, 1)

            def exponent(s, j, zp):
                act.wait_ge(max_ready, s + 1)
                wait(act, turned_ready, 2 * (s - 1))
                act.activation(probs[j % 2][:], scores[j % 2][:].rearrange("p a b -> p (a b)"), ACT.Exp,
                               bias=minus_max[:, j % 2:j % 2 + 1],
                               accum_out=total[:, zp * TILES + j:zp * TILES + j + 1]).then_inc(probs_ready, 1)

            def take_turned(s, C, c, r):
                if r == 0:
                    wait(act, values_ready, C - 1)
                for h in range(2):
                    act.wait_ge(turned_ready, 2 * s + h + 1)
                    act.copy(pT[c, h][:, :, r * P:(r + 1) * P], turned[:, h, :].rearrange("p (k q) -> p k q", k=KH))\
                        .then_inc((pT_hi_ready if split(h) else pT_ready)[h], 1)

            def high_values(n, p, j):
                h = j % 2
                if j >= 6 and split(h):
                    act.wait_ge(proj_taken, 8 * n + j + 1)
                    wait(act, values_ready, 2 * (n - 2) + 2)
                    act.copy(v[p, h][:], v_sum[:]).then_inc(v_hi_ready, 1)

            def copy_values(C):
                act.wait_ge(values_ready, C + 1)
                wait(act, attn_ready, C)
                act.copy(attnT[:], value_sum[:]).then_inc(attnT_copied, 1)

            def normalise(C, c, k):
                act.wait_ge(rstd_ready, 2 * C + 2)
                if rows_buffer(C, c) == c:
                    wait(act, scattered[c], 16 * 2 * CHUNK * k)
                for t in range(CHUNK):
                    a = act.activation(x1[rows_buffer(C, c)][:, t, 0:D], summed[:, t, :], ACT.Identity,
                                       bias=shift[:, 0, t:t + 1], scale=rstd[:, 0, t:t + 1])
                a.then_inc(x1_ready, 1)

            def exponent_of_logits(C):
                act.wait_ge(mask_ready, C + 1)
                act.activation(expd[:], shifted[:], ACT.Exp).then_inc(exp_ready, 1)

            def take_x1_turned(C):
                act.wait_ge(x1_turned, C + 1)
                wait(act, logits_ready, C)
                act.copy(x1T[:], routing_bank(C)).then_inc(x1T_ready, 1)

            def route(C, c, r):
                if r == 1 and live(C - 3):
                    exponent_of_logits(C - 3)
                if r == 2 and live(C - 2):
                    take_x1_turned(C - 2)
                if r == 3 and live(C - 1):
                    copy_values(C - 1)

            def batch(n, p, score_next=True, project_next=True):
                for j in range(TILES):
                    c, r = j // CHUNK, j % CHUNK
                    s, C = TILES * n + j, 2 * n + c
                    if r == 2 and live(C - 2):
                        normalise(C - 2, c, n - 1)
                    if r == 1:
                        take_turned(s, C, c, r)
                    if project_next:
                        project(n + 1, 1 - p, j)
                    if r != 1:
                        take_turned(s, C, c, r)
                    if j < TILES - 1:
                        exponent(s + 1, j + 1, p)
                    elif score_next:
                        exponent(s + 1, 0, 1 - p)
                    if project_next:
                        high_values(n + 1, 1 - p, j)
                    route(C, c, r)

            for j in range(TILES):
                project(0, 0, j)
                high_values(0, 0, j)
            exponent(0, 0, 0)
            batch(0, 0)
            batch(1, 1)
            with act.Fori(0, BATCH_LOOPS) as i:
                batch(2 * i + 2, 0)
                batch(2 * i + 3, 1)
            batch(NB - 2, 0)
            batch(NB - 1, 1, score_next=False, project_next=False)
            B, A = CHUNKS - 2, CHUNKS - 1
            exponent_of_logits(B - 1)
            normalise(B, 0, NB - 1)
            copy_values(A)
            take_x1_turned(B)
            normalise(A, 1, NB - 1)
            take_x1_turned(A)
            exponent_of_logits(B)
            exponent_of_logits(A)

            act.preload_act_table(ACT.Gelu)
            act.wait_ge(table_ready, 1)
            registers = expert_registers(act, "expert", 1)

            def take_rows(g):
                act.wait_ge(in_turned, g.number + 1)
                wait(act, hidden_ready, g.number - 1)
                act.copy(inT[g.parity][:], scores[g.parity][:, 0, :]).then_inc(inT_ready, 1)

            def gelu(g, experts):
                p = g.parity
                act.wait_ge(norm_turned, g.number + 1)
                for t in range(CHUNK):
                    a = act.activation(actT[p][:, t * P:(t + 1) * P], turned[:, p, t * P:(t + 1) * P], ACT.Gelu,
                                       bias=g_cols[:, 1, bass.ds(experts[t], 1)],
                                       scale=g_cols[:, 0, bass.ds(experts[t], 1)])
                a.then_inc(actT_ready, 1)

            def weigh_results(g):
                p = g.parity
                act.wait_ge(result_ready, g.number + 1)
                act.wait_ge(gate_ready, g.number + 1)
                if not isinstance(g.number, int) or g.number >= 2:
                    act.wait_ge(delivered[p], 16 * CHUNK * g.pairs)
                src = (value_sum, work)[p]
                for t in range(CHUNK):
                    a = act.activation(row_out[p][:, t, :], src[:, t * D:(t + 1) * D], ACT.Copy,
                                       scale=gate[g.quarter][:, t:t + 1])
                a.then_inc(result_taken, 1)

            def expert_step(g):
                if g.ahead(-2).within(GROUPS):
                    weigh_results(g.ahead(-2))
                last = g.ahead(-1)
                if last.within(GROUPS):
                    gelu(last, load_experts(act, registers, last.number))
                if g.ahead(2).within(GROUPS):
                    take_rows(g.ahead(2))

            walk_groups(act, GROUPS, expert_step, 2, 2)

            def final_rows(k, fours, q):
                act.wait_ge(shift_ready, k + 1)
                wait(act, final_out[q], 16 * fours)
                for t in range(CHUNK):
                    a = act.activation(final[q][:, t, :], x1_all[:, bass.ds(k, 1), t, :].rearrange("p a d -> p (a d)"),
                                       ACT.Identity, bias=shift[:, q, t:t + 1], scale=rstd[:, q, t:t + 1])
                a.then_inc(final_ready, 1)
                act.wait_ge(final_ready, k + 1)
                act.dma_start(out_v[2 * fours + q // 2][q % 2], final[q][:]).then_inc(final_out[q], 16)

            walk_chunks(act, final_rows)

        @block.vector
        def _(dve):
            chain = Chain(dve, dve_chain)
            then, sync = chain.then, chain.sync

            def hold():
                dve.sem_inc(dve_held, 1)

            dve.wait_ge(iota_done, 2)
            then(dve.tensor_copy(column[:], iota_i[:, 0:P]))
            then(dve.tensor_copy(partition[:], iota_i[:, P:P + 1]))
            then(dve.tensor_copy(expert_ids[:], iota_i[:, 0:E]))
            sync()
            dve.tensor_scalar(ident[:], column[:], partition[:, 0:1], None, ALU.is_equal).then_inc(ident_ready, 1)
            then(dve.tensor_scalar(before[:], column[:], partition[:, 0:1], None, ALU.is_gt))
            then(dve.memset(ones[:], 1.0))
            then(dve.memset(picked_h[:], 0.0))
            then(dve.tensor_scalar(region_start[:], expert_ids[:], float(REGION), None, ALU.mult))
            sync()
            then(dve.tensor_copy(base[:, 0, :], region_start[:]))
            for c in range(2):
                for t in range(CHUNK):
                    then(dve.tensor_scalar(row_ids[:, c, t:t + 1], partition[:], 2.0 * TILES,
                                           2.0 * (CHUNK * c + t), ALU.mult, ALU.add))
            sync()
            dve.wait_ge(setup_pe, 1)
            then(dve.tensor_scalar(wT[:, 0, :], work[:, 0:D], SCALE, None, ALU.mult))
            then(dve.tensor_copy(wT[:, 1, :], work[:, D:2 * D]))
            dve.tensor_copy(woutT[:], work[:, 2 * D:3 * D]).then_inc(setup_dve, 1)
            dve.wait_ge(consts_in, 96)
            then(dve.tensor_scalar(bq[:], bq[:], SCALE, None, ALU.mult))
            dve.tensor_scalar(bv_cols[:], ones[:], bv[:, 0:1], None, ALU.mult).then_inc(setup_dve, 1)
            sync()

            def take_values_setup():
                dve.wait_ge(setup_pe, 2)
                dve.tensor_copy(wvo[:], value_sum[:, 0:D]).then_inc(setup_dve, 1)
                dve.tensor_tensor(bvo_bc[:], value_sum[:, D:2 * D], bout_bc[:], ALU.add).then_inc(setup_dve, 1)
                dve.tensor_copy(g_cols[:], value_sum[:, 2 * D:2 * D + 2 * E].rearrange("p (a e) -> p a e", a=2))\
                    .then_inc(setup_dve, 1)
                dve.wait_ge(setup_dve, 5)

            def project(n, p, j):
                h, bank = j % 2, projection_bank(n, j)
                cols = slice(h * CW, (h + 1) * CW)
                if 2 <= j < 6:
                    k = (j - 2) // 2
                    dve.wait_ge(proj_split, 4 * n + j - 1)
                    dve.scalar_tensor_tensor(out=qkT_lo[p][k][:, cols], in0=bank[:], scalar=(bq, bk)[k][:, 0:1],
                                             in1=qkT_hi[p][k][:, cols].bitcast(F32), op0=ALU.add,
                                             op1=ALU.subtract).then_inc(proj_taken, 1)
                elif j >= 6:
                    dve.wait_ge(proj_filled, 8 * n + j + 1)
                    if split(h):
                        wait(dve, v_ready, len(SPLIT) * n + SPLIT.index(h))
                    else:
                        wait(dve, values_ready, 2 * (n - 2) + 2)
                    dve.tensor_tensor((v_sum if split(h) else v[p, h])[:],
                                      bank[:].rearrange("p (t d) -> p t d", t=KH),
                                      bvo_bc[:].rearrange("p (a d) -> p a d", a=1).to_broadcast([P, KH, D]),
                                      ALU.add).then_inc(proj_taken, 1)

            def low_values(n, p, j):
                h = j % 2
                if j >= 6 and split(h):
                    dve.wait_ge(v_hi_ready, len(SPLIT) * n + SPLIT.index(h) + 1)
                    wait(dve, values_ready, 2 * (n - 2) + 2)
                    dve.tensor_tensor(v_lo[p, h][:], v_sum[:], v[p, h][:].bitcast(F32),
                                      ALU.subtract).then_inc(v_ready, 1)

            def low_turned(s, C, c, r, h):
                if split(h):
                    if r == 0:
                        wait(dve, values_ready, C - 1)
                    dve.wait_ge(pT_hi_ready[h], s + 1)
                    dve.tensor_tensor(pT_lo[c, h][:, :, r * P:(r + 1) * P],
                                      turned[:, h, :].rearrange("p (k q) -> p k q", k=KH),
                                      pT[c, h][:, :, r * P:(r + 1) * P].bitcast(F32),
                                      ALU.subtract).then_inc(pT_ready[h], 1)

            def maximum(s, j):
                dve.wait_ge(scores_ready, s + 1)
                dve.tensor_reduce(minus_max[:, j % 2:j % 2 + 1], scores[j % 2][:], AX.XY, ALU.max,
                                  negate=True).then_inc(max_ready, 1)

            def attention_rows(C, c, zp, k):
                z = zp * TILES + c * CHUNK
                then(dve.reciprocal(inv_total[:], total[:, z:z + CHUNK]))
                sync()
                bank = routing_bank(C)
                dve.wait_ge(attn_ready, C + 1)
                dve.wait_ge(res_in[c], 16 * (k + 1))
                wait(dve, x1_ready, C)
                for t in range(CHUNK):
                    a = dve.scalar_tensor_tensor(out=summed[:, t, :], in0=bank[:, t * P:(t + 1) * P],
                                                 scalar=inv_total[:, t:t + 1], in1=x_res[c][:, t, :],
                                                 op0=ALU.mult, op1=ALU.add)
                    if t == CHUNK - 1:
                        a.then_inc(attn_taken, 1)
                dve.wait_ge(attn_taken, C + 1)
                for t in range(CHUNK):
                    then(dve.bn_stats(stats[:, 0, t, :], summed[:, t, :]))
                sync()
                hold()
                for t in range(CHUNK):
                    then(dve.bn_aggr(mean_var[:, 0, t, :], stats[:, 0, t, :]))
                sync()
                then(dve.tensor_scalar(minus_mean[:, 0, :], mean_var[:, 0, :, 0], -1.0, None, ALU.mult))
                dve.tensor_scalar(var[:, 0, :], mean_var[:, 0, :, 1], EPS, None, ALU.add)\
                    .then_inc(var_ready, 1)

            def pick_experts(C, c):
                bank = routing_bank(C)
                dve.wait_ge(logits_ready, C + 1)
                dve.tensor_tensor(logits[:], bank[:, 0:CHUNK * E].rearrange("p (t e) -> p t e", t=CHUNK),
                                  br_bc[:].rearrange("p (a e) -> p a e", a=1).to_broadcast([P, CHUNK, E]),
                                  ALU.add).then_inc(logits_taken, 1)
                dve.wait_ge(logits_taken, C + 1)
                hold()
                for t in range(CHUNK):
                    then(dve.max(top[:, t, :], logits[:, t, :]))
                sync()
                hold()
                for t in range(CHUNK):
                    then(dve.max_index(top_i[:, t, :], top[:, t, :], logits[:, t, :]))
                largest = top[:, :, 0:1]
                then(dve.tensor_tensor(shifted[:, :, 0:E], logits[:], largest.to_broadcast([P, CHUNK, E]),
                                       ALU.subtract))
                then(dve.tensor_tensor(shifted[:, :, E:E + 2], top[:, :, 0:2],
                                       largest.to_broadcast([P, CHUNK, 2]), ALU.subtract))
                sync()
                then(dve.tensor_copy(top_f[:], top_i[:, :, 0:2]))
                sync()
                ids = expert_ids[:].rearrange("p (a e) -> p a e", a=1).to_broadcast([P, CHUNK, E])
                for s in range(2):
                    then(dve.tensor_tensor(picked[:, s], ids, top_f[:, :, s:s + 1].to_broadcast([P, CHUNK, E]),
                                           ALU.is_equal))
                sync()
                dve.tensor_tensor(picked_h[:, 0:CHUNK, :], picked[:, 0], picked[:, 1], ALU.add).then_inc(mask_ready, 1)

            def take_ranks(C, c):
                bank = routing_bank(C)
                dve.wait_ge(rank_ready, C + 1)
                then(dve.tensor_tensor(base[:, 1 - c, :], base[:, c, :], bank[:, CHUNK * E:(CHUNK + 1) * E], ALU.add))
                dve.tensor_tensor(rank[:], bank[:, 0:CHUNK * E].rearrange("p (t e) -> p t e", t=CHUNK),
                                  base[:, c:c + 1, :].to_broadcast([P, CHUNK, E]), ALU.add).then_inc(rank_taken, 1)

            def place_rows(C, c):
                dve.wait_ge(exp_ready, C + 1)
                then(dve.tensor_reduce(gate_sum[:, 0, :], expd[:, :, 0:E], AX.X, ALU.add))
                dve.wait_ge(rank_taken, C + 1)
                for s in range(2):
                    then(dve.tensor_tensor(rank_k[:, s], picked[:, s], rank[:], ALU.mult))
                sync(behind=2)
                then(dve.reciprocal(gate_sum[:, 1, :], gate_sum[:, 0, :]))
                rows = x1[rows_buffer(C, c)]
                then(dve.tensor_copy(rows[:, :, D:D + 1], row_ids[:, c, :].rearrange("p (t a) -> p t a", a=1)))
                then(dve.tensor_copy(rows[:, :, D + 1:D + 2], top_f[:, :, 1:2]))
                sync(behind=2)
                then(dve.tensor_tensor(gate_p[:], expd[:, :, E:E + 2],
                                       gate_sum[:, 1, :].rearrange("p (t a) -> p t a", a=1).to_broadcast([P, CHUNK, 2]),
                                       ALU.mult))
                then(dve.tensor_reduce(place_f[:], rank_k[:], AX.X, ALU.add))
                sync(behind=1)
                then(dve.tensor_reduce(gate_sum[:, 2, :], gate_p[:], AX.X, ALU.add))
                sync(behind=1)
                then(dve.tensor_copy(place[rows_buffer(C, c)][:], place_f[:]))
                sync(behind=1)
                then(dve.tensor_scalar(gate_sum[:, 2, :], gate_sum[:, 2, :], 1e-9, None, ALU.max))
                then(dve.tensor_scalar(row_ids[:, c, :], row_ids[:, c, :], 2.0 * S, None, ALU.add))
                sync(behind=1)
                then(dve.reciprocal(gate_sum[:, 3, :], gate_sum[:, 2, :]))
                sync()
                dve.tensor_tensor(rows[:, :, D + 2:D + 4], gate_p[:],
                                  gate_sum[:, 3, :].rearrange("p (t a) -> p t a", a=1).to_broadcast([P, CHUNK, 2]),
                                  ALU.mult).then_inc(place_ready, 1)

            def route_before(C, c, r, zp, k):
                if r == 0 and live(C - 3):
                    pick_experts(C - 3, 1 - c)
                if r == 1 and live(C - 2):
                    attention_rows(C - 2, c, zp, k)
                if r == 2 and live(C - 3):
                    take_ranks(C - 3, 1 - c)

            def route_after(C, c, r):
                if r == 2 and live(C - 3):
                    place_rows(C - 3, 1 - c)

            def batch(n, p, score_next=True, project_next=True):
                for j in range(TILES):
                    c, r = j // CHUNK, j % CHUNK
                    s, C = TILES * n + j, 2 * n + c
                    route_before(C, c, r, 1 - p, n - 1)
                    low_turned(s, C, c, r, 0)
                    if j < TILES - 1:
                        maximum(s + 1, j + 1)
                    elif score_next:
                        maximum(s + 1, 0)
                    if project_next:
                        project(n + 1, 1 - p, j)
                    low_turned(s, C, c, r, 1)
                    route_after(C, c, r)
                    if project_next:
                        low_values(n + 1, 1 - p, j)

            for j in range(TILES):
                if j == 6:
                    take_values_setup()
                project(0, 0, j)
                low_values(0, 0, j)
            maximum(0, 0)
            dve.wait_ge(pool_const, 3)
            then(dve.memset(pad_row[:, D:D + 1], 2.0 * N))
            then(dve.memset(pad_row[:, D + 1:D + 2], -1.0))
            steps_of_chunk = 37
            batch(0, 0)
            batch(1, 1)
            with dve.Fori(0, BATCH_LOOPS) as i:
                chain.enter(4 * steps_of_chunk, i)
                batch(2 * i + 2, 0)
                batch(2 * i + 3, 1)
            chain.leave(BATCH_LOOPS)
            batch(NB - 2, 0)
            batch(NB - 1, 1, score_next=False, project_next=False)
            B, A = CHUNKS - 2, CHUNKS - 1
            pick_experts(B - 1, 1)
            attention_rows(B, 0, 1, NB - 1)
            take_ranks(B - 1, 1)
            place_rows(B - 1, 1)
            attention_rows(A, 1, 1, NB - 1)
            pick_experts(B, 0)
            take_ranks(B, 0)
            place_rows(B, 0)
            pick_experts(A, 1)
            take_ranks(A, 1)
            place_rows(A, 1)

            sync()
            end = base[:, 0, :]
            dve.tensor_copy(base_i[:], end).then_inc(pad_ready, 1)
            count, count_i = tab[:, 0, :], tab_i
            then(dve.tensor_tensor(count, end, region_start[:], ALU.subtract))
            sync()
            then(dve.tensor_scalar(count, count, float(P - 1), None, ALU.add))
            sync()
            then(dve.tensor_copy(count_i[:], count))
            sync()
            then(dve.tensor_scalar(count_i[:], count_i[:], 7, None, ALU.logical_shift_right))
            sync()
            tiles = tab[:, 1, :]
            then(dve.tensor_copy(tiles, count_i[:]))
            upto = [tab[:, 2, :], tab[:, 3, :]]
            then(dve.tensor_copy(upto[0], count_i[:]))
            w = 1
            while w < E:
                sync()
                then(dve.tensor_tensor(upto[1][:, w:E], upto[0][:, w:E], upto[0][:, 0:E - w], ALU.add))
                then(dve.tensor_copy(upto[1][:, 0:w], upto[0][:, 0:w]))
                upto.reverse()
                w *= 2
            sync()
            for i in range(2):
                then(dve.tensor_scalar(tab[:, 4 + i, 0:1], partition[:], float(i * P), None, ALU.add))
            sync()
            for i in range(2):
                then(dve.tensor_scalar(per_tile[:, i, :], upto[0], tab[:, 4 + i, 0:1], None, ALU.is_le))
            sync()
            then(dve.tensor_tensor(per_tile2[:], per_tile[:],
                                   tiles.rearrange("p (a e) -> p a e", a=1).to_broadcast([P, 2, E]), ALU.mult))
            then(dve.tensor_reduce(tile_cols[:, 0:2], per_tile[:], AX.X, ALU.add))
            sync()
            then(dve.tensor_reduce(tab[:, 6, 0:2], per_tile2[:], AX.X, ALU.add))
            sync()
            for i in range(2):
                then(dve.tensor_tensor(tab[:, 7, i:i + 1], tab[:, 4 + i, 0:1], tab[:, 6, i:i + 1], ALU.subtract))
            sync()
            then(dve.tensor_scalar(tab[:, 7, 0:2], tab[:, 7, 0:2], float(P), None, ALU.mult))
            sync()
            then(dve.scalar_tensor_tensor(out=tab[:, 6, 0:2], in0=tile_cols[:, 0:2], scalar=float(REGION),
                                          in1=tab[:, 7, 0:2], op0=ALU.mult, op1=ALU.add))
            sync()
            dve.tensor_scalar(tile_cols[:, 2:4], tab[:, 6, 0:2], base[:, 0, E - 1:E], None,
                              ALU.min).then_inc(cols_ready, 1)
            dve.tensor_scalar(tile_cols[:, 0:2], tile_cols[:, 0:2], float(E - 1), None,
                              ALU.min).then_inc(cols_ready, 1)
            dve.wait_ge(cols_ready, 2)
            for i in range(2):
                dve.tensor_scalar(expert_cols[:, i, :], ones[:], tile_cols[:, i:i + 1], None,
                                  ALU.mult).then_inc(cols_ready, 1)
            dve.wait_ge(table_pe, 1)
            dve.tensor_copy(tile_table[:], work[0:1, :]).then_inc(table_ready, 1)
            dve.wait_ge(table_pe, 2)
            then(dve.tensor_copy(expert_of_tile[:], value_sum[:, 0:2 * P]))
            dve.wait_ge(table_ready, 1)
            dve.wait_ge(expert_in, 64)
            sync()
            registers = expert_registers(dve, "expert", 1)

            def hidden_rows(g, experts):
                p, q = g.parity, g.quarter
                dve.wait_ge(hidden_ready, g.number + 1)
                wait(dve, normed_ready, g.number - 1)
                for t in range(CHUNK):
                    then(dve.tensor_tensor(hidden[p][:, t, :], scores[p][:, 1, t * H:(t + 1) * H],
                                           b1_bc[:, bass.ds(experts[t], 1), :].rearrange("p a h -> p (a h)"), ALU.add))
                column_of = lambda i: row_in[q][:, :, D + i]
                then(dve.tensor_tensor(is_second[:], column_of(1),
                                       expert_of_tile[:, bass.ds(g.number * CHUNK, CHUNK)], ALU.is_equal))
                sync(behind=1)
                for t in range(CHUNK):
                    then(dve.bn_stats(stats[:, p, t, :], hidden[p][:, t, :]))
                sync(behind=CHUNK)
                then(dve.tensor_tensor(dest_f[:], is_second[:], column_of(0), ALU.add))
                then(dve.tensor_tensor(gate_part[:, 0, :], is_second[:], column_of(3), ALU.mult))
                then(dve.tensor_tensor(gate_part[:, 1, :], is_second[:], column_of(2), ALU.mult))
                sync(behind=3)
                hold()
                for t in range(CHUNK):
                    then(dve.bn_aggr(mean_var[:, p, t, :], stats[:, p, t, :]))
                sync(behind=CHUNK)
                if not isinstance(g.number, int) or g.number >= 4:
                    dve.wait_ge(delivered[p], 16 * CHUNK * (g.pairs - 1))
                then(dve.tensor_copy(dest[q][:], dest_f[:]))
                then(dve.tensor_tensor(gate_part[:, 2, :], column_of(2), gate_part[:, 1, :], ALU.subtract))
                sync(behind=2)
                dve.tensor_scalar(var[:, p, :], mean_var[:, p, :, 1], EPS, None, ALU.add).then_inc(hidden_var_ready, 1)
                sync()
                dve.tensor_tensor(gate[q][:], gate_part[:, 0, :], gate_part[:, 2, :], ALU.add).then_inc(gate_ready, 1)

            def norm_rows(g):
                p = g.parity
                dve.wait_ge(hidden_scale_ready, g.number + 1)
                wait(dve, norm_turned, g.number - 1)
                for t in range(CHUNK):
                    a = dve.tensor_scalar(normed[p][:, t, :], hidden[p][:, t, :], mean_var[:, p, t, 0:1],
                                          rstd[:, p, t:t + 1], ALU.subtract, ALU.mult)
                a.then_inc(normed_ready, 1)

            def expert_step(g):
                if g.within(GROUPS):
                    experts = load_experts(dve, registers, g.number)
                if g.ahead(-1).within(GROUPS):
                    norm_rows(g.ahead(-1))
                if g.within(GROUPS):
                    hidden_rows(g, experts)

            per_step = 3 * CHUNK + 6
            walk_groups(dve, GROUPS, expert_step, 0, 1,
                        enter=lambda i: chain.enter(4 * per_step, i), leave=chain.leave)

            def final_rows(k):
                return x1_all[:, bass.ds(k, 1), :, :].rearrange("p a t d -> p (a t) d")

            def final_step(k, fours, q):
                first, c = isinstance(k, int) and k < 2, q % 2
                rows = final_rows(k)
                dve.wait_ge(pair_mixed, k + 1)
                dve.tensor_tensor(rows, mixed[c][:], rows, ALU.add).then_inc(row_total, 1)
                dve.wait_ge(row_total, k + 1)
                sync()
                hold()
                for t in range(CHUNK):
                    then(dve.bn_stats(stats[:, c, t, :], rows[:, t, :]))
                if not first:
                    final_shift(k - 2, (q - 2) % 4)
                sync()
                hold()
                for t in range(CHUNK):
                    then(dve.bn_aggr(mean_var[:, c, t, :], stats[:, c, t, :]))
                sync()
                dve.tensor_scalar(var[:, c, :], mean_var[:, c, :, 1], EPS, None, ALU.add).then_inc(final_var_ready, 1)
                wait(dve, shift_ready, k - 1)
                then(dve.tensor_scalar(minus_mean[:, c, :], mean_var[:, c, :, 0], -1.0, None, ALU.mult))

            def final_shift(k, q):
                dve.wait_ge(final_scale_ready, k + 1)
                wait(dve, final_ready, k - 3)
                dve.tensor_tensor(shift[:, q, :], minus_mean[:, q % 2, :], rstd[:, q, :],
                                  ALU.mult).then_inc(shift_ready, 1)

            walk_chunks(dve, final_step, enter=lambda i: chain.enter(4 * (2 * CHUNK + 1), i), leave=chain.leave)
            sync()
            for k in (CHUNKS - 2, CHUNKS - 1):
                final_shift(k, k % 4)


_INS = ["L0_attn_x", "L0_attn_w_q", "L0_attn_b_q", "L0_attn_w_k", "L0_attn_b_k", "L0_attn_w_v", "L0_attn_b_v",
        "L0_attn_w_out", "L0_attn_b_out", "L0_ffn_Wr", "L0_ffn_br", "L0_ffn_W1", "L0_ffn_b1", "L0_ffn_g1",
        "L0_ffn_be1", "L0_ffn_W2", "L0_ffn_b2"]


def kernel(**inputs):
    import numpy as _np
    import concourse.bacc as _bacc
    from concourse import mybir as _mybir
    from concourse.bass_utils import run_bass_kernel_spmd as _run

    nc = _bacc.Bacc("TRN2", target_bir_lowering=False, num_devices=1)
    arrays, args = {}, []
    for name in _INS:
        a = _np.ascontiguousarray(inputs[name])
        arrays[f"in_{name}_dram"] = a
        args.append(nc.dram_tensor(f"in_{name}_dram", a.shape, _mybir.dt.from_np(a.dtype), kind="ExternalInput").ap())
    shape = inputs["L0_attn_x"].shape
    out = nc.dram_tensor("out_0_dram", shape, _mybir.dt.float32, kind="ExternalOutput").ap()
    post_ln_moe_layer(nc, *args, out)
    r = _run(nc, [arrays], core_ids=[0])
    return r.results[0]["out_0_dram"]
```
